# Optimizing a Trainium2 kernel written in Bass

```python
import numpy as np
import jax
import jax.numpy as jnp

def _softmax(x, axis=-1):
    return jax.nn.softmax(x, axis=axis)

def _gelu(x):
    return jax.nn.gelu(x, approximate=True)

def _silu(x):
    return jax.nn.silu(x)

def _sigmoid(x):
    return jax.nn.sigmoid(x)

def _layernorm(x, axis=-1, eps=1e-05):
    m = jnp.mean(x, axis=axis, keepdims=True)
    v = jnp.var(x, axis=axis, keepdims=True)
    return (x - m) / jnp.sqrt(v + eps)

def _scatter_add(tgt, idx, src, axis=0):
    return tgt.at[idx].add(src)

def _segment_sum(src, seg, n):
    return jax.ops.segment_sum(src, seg, n)
kernel_name = 'mk_sandwich_d1_jaxref_r4_e963f2'

def setup_inputs(seed: int=0):
    np.random.seed(seed)
    _w = jnp.asarray

    def _L0_attn_setup():
        import jax, jax.numpy as jnp
        import numpy as np
        NUM_HEADS = 32
        HIDDEN = 512
        HEAD_DIM = HIDDEN // NUM_HEADS
        BATCH = 2
        SEQ = 512
        STD = 0.02

        def _split_heads(x):
            b, s, _ = x.shape
            return x.reshape(b, s, NUM_HEADS, HEAD_DIM).transpose(0, 2, 1, 3)
        key = jax.random.key(seed)
        ks = jax.random.split(key, 9)

        def w(k):
            return jax.random.normal(k, (HIDDEN, HIDDEN), dtype=jnp.float32) * STD
        return {'hidden_states': jax.random.normal(ks[0], (BATCH, SEQ, HIDDEN), dtype=jnp.float32), 'Wq': w(ks[1]), 'bq': jnp.zeros((HIDDEN,), jnp.float32), 'Wk': w(ks[2]), 'bk': jnp.zeros((HIDDEN,), jnp.float32), 'Wv': w(ks[3]), 'bv': jnp.zeros((HIDDEN,), jnp.float32), 'Wo': w(ks[4]), 'bo': jnp.zeros((HIDDEN,), jnp.float32)}
    _L0_attn_in = _L0_attn_setup()

    def _L0_ffn_setup():
        import jax, jax.numpy as jnp
        import numpy as np
        B, S, H, I = (1, 64, 512, 1536)

        def _quantized_matmul(x, w, scale):
            wq = w.astype(jnp.float8_e4m3fn).astype(x.dtype)
            y = jnp.einsum('bsi,io->bso', x, wq)
            return y * scale
        key = jax.random.key(seed)
        ks = jax.random.split(key, 7)
        return {'x': jax.random.normal(ks[0], (B, S, H), dtype=jnp.float32), 'gate_w': jax.random.normal(ks[1], (H, I), dtype=jnp.float32) * 0.02, 'up_w': jax.random.normal(ks[2], (H, I), dtype=jnp.float32) * 0.02, 'down_w': jax.random.normal(ks[3], (I, H), dtype=jnp.float32) * 0.02, 'gate_scale': jax.random.uniform(ks[4], (I,), dtype=jnp.float32, minval=0.5, maxval=1.5), 'up_scale': jax.random.uniform(ks[5], (I,), dtype=jnp.float32, minval=0.5, maxval=1.5), 'down_scale': jax.random.uniform(ks[6], (H,), dtype=jnp.float32, minval=0.5, maxval=1.5)}
    _L0_ffn_in = _L0_ffn_setup()
    _d = {'L0_attn_hidden_states': _L0_attn_in['hidden_states'], 'L0_attn_Wq': _L0_attn_in['Wq'], 'L0_attn_bq': _L0_attn_in['bq'], 'L0_attn_Wk': _L0_attn_in['Wk'], 'L0_attn_bk': _L0_attn_in['bk'], 'L0_attn_Wv': _L0_attn_in['Wv'], 'L0_attn_bv': _L0_attn_in['bv'], 'L0_attn_Wo': _L0_attn_in['Wo'], 'L0_attn_bo': _L0_attn_in['bo'], 'L0_ffn_gate_w': _L0_ffn_in['gate_w'], 'L0_ffn_up_w': _L0_ffn_in['up_w'], 'L0_ffn_down_w': _L0_ffn_in['down_w'], 'L0_ffn_gate_scale': _L0_ffn_in['gate_scale'], 'L0_ffn_up_scale': _L0_ffn_in['up_scale'], 'L0_ffn_down_scale': _L0_ffn_in['down_scale']}
    _x0 = _d['L0_attn_hidden_states']
    _d['L0_attn_hidden_states'] = jax.random.normal(jax.random.fold_in(jax.random.key(seed), 1), (8, 512, 512), dtype=_x0.dtype)
    del _x0
    return _d

def reference(L0_attn_hidden_states, L0_attn_Wq, L0_attn_bq, L0_attn_Wk, L0_attn_bk, L0_attn_Wv, L0_attn_bv, L0_attn_Wo, L0_attn_bo, L0_ffn_gate_w, L0_ffn_up_w, L0_ffn_down_w, L0_ffn_gate_scale, L0_ffn_up_scale, L0_ffn_down_scale):

    def _L0_attn_ref(hidden_states, Wq, bq, Wk, bk, Wv, bv, Wo, bo):
        import jax, jax.numpy as jnp
        import numpy as np
        NUM_HEADS = 32
        HIDDEN = 512
        HEAD_DIM = HIDDEN // NUM_HEADS
        BATCH = 2
        SEQ = 512
        STD = 0.02

        def _split_heads(x):
            b, s, _ = x.shape
            return x.reshape(b, s, NUM_HEADS, HEAD_DIM).transpose(0, 2, 1, 3)
        scale = 1.0 / jnp.sqrt(jnp.float32(HEAD_DIM))
        q = _split_heads(hidden_states @ Wq + bq)
        k = _split_heads(hidden_states @ Wk + bk)
        v = _split_heads(hidden_states @ Wv + bv)
        scores = jnp.einsum('bhqd,bhkd->bhqk', q, k) * scale
        probs = jax.nn.softmax(scores, axis=-1)
        ctx = jnp.einsum('bhqk,bhkd->bhqd', probs, v)
        b, h, s, d = ctx.shape
        ctx = ctx.transpose(0, 2, 1, 3).reshape(b, s, h * d)
        return ctx @ Wo + bo

    def _L0_ffn_ref(x, gate_w, up_w, down_w, gate_scale, up_scale, down_scale):
        import jax, jax.numpy as jnp
        import numpy as np
        B, S, H, I = (1, 64, 512, 1536)

        def _quantized_matmul(x, w, scale):
            wq = w.astype(jnp.float8_e4m3fn).astype(x.dtype)
            y = jnp.einsum('bsi,io->bso', x, wq)
            return y * scale
        gate = jax.nn.silu(_quantized_matmul(x, gate_w, gate_scale))
        up = _quantized_matmul(x, up_w, up_scale)
        fuse = gate * up
        return _quantized_matmul(fuse, down_w, down_scale)
    x = L0_attn_hidden_states
    x = x + _layernorm(_L0_attn_ref(_layernorm(x, axis=-1), L0_attn_Wq, L0_attn_bq, L0_attn_Wk, L0_attn_bk, L0_attn_Wv, L0_attn_bv, L0_attn_Wo, L0_attn_bo), axis=-1)
    x = x + _layernorm(_L0_ffn_ref(_layernorm(x, axis=-1), L0_ffn_gate_w, L0_ffn_up_w, L0_ffn_down_w, L0_ffn_gate_scale, L0_ffn_up_scale, L0_ffn_down_scale), axis=-1)
    return x

_drawn_inputs = setup_inputs


def setup_inputs(seed=0):
    import zlib

    import numpy as np

    out = dict(_drawn_inputs(seed))
    spreads = {'L0_attn_bq': (0.0, 0.8),
     'L0_attn_bk': (0.0, 0.8),
     'L0_attn_bv': (0.0, 0.1),
     'L0_attn_bo': (0.0, 0.1)}
    factors = {'L0_attn_Wq': 2.875, 'L0_attn_Wk': 2.825}
    for name, (base, spread) in spreads.items():
        noise = np.random.default_rng([zlib.crc32(name.encode()), seed]).standard_normal(out[name].shape)
        drawn = base * np.exp(spread * noise) if base else spread * noise
        out[name] = jnp.asarray(drawn.astype(out[name].dtype))
    for name, factor in factors.items():
        out[name] = (out[name] * factor).astype(out[name].dtype)
    return out
```

```python
from contextlib import ExitStack

import concourse.bass as bass
from concourse import mybir

F32 = mybir.dt.float32
F32R = mybir.dt.float32r
F16 = mybir.dt.float16
I32 = mybir.dt.int32
ALU = mybir.AluOpType
ACT = mybir.ActivationFunctionType
AX = mybir.AxisListType

P = 128
NH = 32
D = 16
GH = 4
EPS = 1e-5
SETS = 3
FILL = 9 * 16
LEAD = 6


AGGR = 7


def aggregate(dve, n, T, width, stats, mean, spread, varpe, stat_done, step_done):
    dve.wait_ge(stat_done, n * T + T)
    dve.tensor_tensor(spread[:, 0, :], stats[:, :, 1], stats[:, :, 4], ALU.add).then_inc(step_done, 1)
    dve.tensor_tensor(spread[:, 1, :], stats[:, :, 1], stats[:, :, 4], ALU.subtract).then_inc(step_done, 1)
    dve.tensor_tensor(spread[:, 2, :], stats[:, :, 2], stats[:, :, 5], ALU.add).then_inc(step_done, 1)
    dve.wait_ge(step_done, n * AGGR + 2)
    dve.tensor_scalar(mean[:], spread[:, 0, :], 0.5, None, ALU.mult).then_inc(step_done, 1)
    dve.tensor_tensor(varpe[:], spread[:, 1, :], spread[:, 1, :], ALU.mult).then_inc(step_done, 1)
    dve.wait_ge(step_done, n * AGGR + 5)
    dve.scalar_tensor_tensor(varpe[:], varpe[:], width / 4.0, spread[:, 2, :], ALU.mult, ALU.add).then_inc(step_done, 1)
    dve.wait_ge(step_done, n * AGGR + 6)
    dve.tensor_scalar(varpe[:], varpe[:], 1.0 / width, EPS, ALU.mult, ALU.add).then_inc(step_done, 1)


def layer(nc, x, Wq, bq, Wk, bk, Wv, bv, Wo, bo, gate_w, up_w, down_w, gate_s, up_s, down_s, out):
    with ExitStack() as ctx:
        middle = nc.dram_tensor("middle_rows", list(x.shape), F32, kind="Internal").ap()
        ident = ctx.enter_context(nc.sbuf_tensor("ident", [P, P], F32))
        with ExitStack() as inner:
            attention_pass(nc, inner, ident, x, Wq, bq, Wk, bk, Wv, bv, Wo, bo, middle)
        with ExitStack() as inner:
            ffn_pass(nc, inner, ident, middle, gate_w, up_w, down_w, gate_s, up_s, down_s, out)


def attention_pass(nc, ctx, ident, x, Wq, bq, Wk, bk, Wv, bv, Wo, bo, middle):
    B, S, H = x.shape
    T = S // P
    KC = H // P
    G = NH // GH
    O = G // 2
    HEADS = NH
    STEPS = G * T

    sb = lambda name, shape, dt=F32: ctx.enter_context(nc.sbuf_tensor(name, shape, dt))
    ps = lambda name, shape: ctx.enter_context(nc.psum_tensor(name, shape, F32))
    sem = lambda name: ctx.enter_context(nc.semaphore(name))

    w_h = {n: sb(f"w{n}_high", [P, KC, H], F32R) for n in "qkvo"}
    w_l = {n: sb(f"w{n}_low", [P, KC, H], F32R) for n in "qkvo"}
    b_qk = sb("bias_qk", [P, 2, O])
    bv_rows = sb("bias_v_rows", [P, H])
    bo_rows = sb("bias_o_rows", [P, H])
    half_mask = sb("half_mask", [P, 2])
    minus_half = sb("minus_half", [P, T])

    x_rows = sb("x_rows", [P, T, H])
    xT_h = sb("xT_high", [P, KC, S], F32R)
    xT_l = sb("xT_low", [P, KC, S], F32R)
    qkT = sb("qkT", [P, 4, S], F32R)
    v_one = sb("v_one", [P, T, NH, 2 * D])
    q_st = sb("q_stack", [P, SETS * GH, S], F32R)
    k_st = sb("k_stack", [P, SETS * GH, S], F32R)
    probs = sb("probs", [P, 2, GH, S])
    cT_h = sb("ctxT_high", [P, O, S], F32R)
    cT_l = sb("ctxT_low", [P, O, S], F32R)
    ctx_raw = sb("ctx_raw", [P, S])
    den = sb("denominators", [P, S])
    den_inv = sb("den_inverse", [P, S])
    maxima = sb("maxima", [P, 2, GH * T])
    max_h = sb("max_high", [GH * T, 2, P], F32R)
    max_l = sb("max_low", [GH * T, 2, P], F32R)
    stats = sb("stats", [P, T, 6])
    mean = sb("mean", [P, T])
    spread = sb("spread", [P, 3, T])
    varpe = sb("var_plus_eps", [P, T])
    rstd = sb("rstd", [P, T])

    xn = probs[:, 0]
    y = probs[:, 1]

    rot = [ps(f"rot{i}", [P, S]) for i in range(2)]
    work = ps("work", [P, 4, S])
    cps = [ps(f"ctx{i}", [P, S]) for i in range(2)]

    w_in = {n: sem(f"w{n}_in") for n in "qkvo"}
    b_in = sem("biases_in")
    w_split = sem("w_split")
    w_high = sem("w_high")
    q_scaled = sem("q_scaled")
    const_a = sem("const_made")
    const_v = sem("masks_made")
    x_in = sem("x_in")
    ln_stat = sem("ln_stat")
    ln_aggr = sem("ln_aggr")
    ln_rstd = sem("ln_rstd")
    xn_ready = sem("xn_ready")
    xT_ps = sem("xT_in_psum")
    xTh = sem("xT_high_ready")
    xTl = sem("xT_low_ready")
    v_ps = sem("v_in_psum")
    v_ready = sem("v_ready")
    rot_full = sem("rot_full")
    rot_free = sem("rot_free")
    qk_h = sem("qk_high_ready")
    stack_in = [sem(f"stack_in{i}") for i in range(SETS)]
    maxh = sem("max_high_ready")
    m_in = [sem(f"max_rows_in{i}") for i in range(2)]
    st_full = sem("scores_in_psum")
    p_full = sem("probs_ready")
    pv_done = sem("pv_done")
    c0_out = sem("ctx0_read")
    c1_out = sem("ctx1_read")
    den_sh = sem("den_shuffled")
    den_ln = sem("den_ln")
    den_rec = sem("den_inverse_ready")
    c_norm = sem("ctx_normalised")
    c_h = sem("ctx_high_ready")
    c_l = sem("ctx_low_ready")
    o_ps = sem("out_in_psum")
    y_ready = sem("y_ready")
    yn_ready = sem("y_normalised")
    r_ready = sem("row_sum_ready")
    rows_out = sem("rows_out")

    def unit(h):
        return [("s", h // GH, h % GH, qc) for qc in range(T)]

    ahead = {}
    before = [("q", 0), ("k", 0)] + ([("q", 1), ("k", 1)] if O > 1 else [])
    for h in range(LEAD):
        if h and h % GH == 0:
            before.append(("t", h // GH - 1))
        before += unit(h)
    for n in range(STEPS):
        items = []
        h = n + LEAD
        if h % GH == 0 and h <= HEADS:
            items.append(("t", h // GH - 1))
        if h < HEADS:
            items += unit(h)
        g, c = divmod(n, T)
        if g % 2 == 1 and c in (2, 3) and (g + 3) // 2 < O:
            items.append(("qk"[c - 2], (g + 3) // 2))
        ahead[n] = items
    order = before + [i for n in range(STEPS) for i in ahead[n]]
    place = {item: i for i, item in enumerate(order)}
    ROT = len(order)
    assert ROT == 2 * O + NH * T + G and ROT % 2 == 0

    def slots(g):
        s = g % SETS
        return slice(s * GH, s * GH + GH)

    def free_steps(g):
        return (g - SETS + 1) * T if g >= SETS else 0

    fills = [len([g for g in range(G) if g % SETS == s]) for s in range(SETS)]

    block = ctx.enter_context(nc.Block())

    @block.sync
    def _(sp):
        def load_weight(n, W, slot):
            dst = probs[:, slot]
            if n == "o":
                v = W.rearrange("(o e j d) n -> j e d o n", o=O, e=2, j=GH)
                for j in range(GH):
                    for e in range(2):
                        lo = 32 * j + D * e
                        sp.dma_start(dst[lo:lo + D, :, :], v[j, e]).then_inc(w_in[n], 16)
            else:
                sp.dma_start(dst, W.rearrange("(c p) n -> p c n", p=P)).then_inc(w_in[n], 16)

        load_weight("q", Wq, 0)
        load_weight("k", Wk, 1)
        for i, bias in enumerate((bq, bk)):
            v = bias.rearrange("(o g h d) -> g d h o", o=O, g=2, h=GH)
            for g in range(2):
                for d in range(D):
                    lo = 64 * g + GH * d
                    sp.dma_start(b_qk[lo:lo + GH, i, :], v[g, d], allow_slow_non_contiguous=True).then_inc(b_in, 16)
        sp.dma_start(bv_rows[:], bv.partition_broadcast(P)).then_inc(b_in, 16)
        sp.dma_start(bo_rows[:], bo.partition_broadcast(P)).then_inc(b_in, 16)
        sp.wait_ge(w_split, 1)
        load_weight("v", Wv, 0)
        sp.wait_ge(w_split, 2)
        load_weight("o", Wo, 1)

        with sp.Fori(0, B) as b:
            def fill(g):
                half = slice(64 * (g % 2), 64 * (g % 2) + 64)
                sp.wait_ge(rot_free, b * ROT + place[("k", g // 2)] + 1)
                sp.wait_ge(st_full, (b * STEPS + free_steps(g)) * 2)
                sp.dma_start(q_st[64:66, slots(g), :].bitcast(F32), k_st[96:98, slots(g), :].bitcast(F32)).then_inc(stack_in[g % SETS], 16)
                for r, (qp, kp) in enumerate(((0, 2), (0, 3), (1, 2), (1, 3))):
                    rows = slice(D * r, D * r + D)
                    sp.dma_start(q_st[rows, slots(g), :].bitcast(F32), qkT[half, qp, :].bitcast(F32)).then_inc(stack_in[g % SETS], 16)
                    sp.dma_start(k_st[rows, slots(g), :].bitcast(F32), qkT[half, kp, :].bitcast(F32)).then_inc(stack_in[g % SETS], 16)

            def max_rows(g):
                sp.wait_ge(rot_free, b * ROT + place[("t", g)] + 1)
                for r, part in enumerate((max_h, max_l)):
                    sp.dma_start(q_st[64 + r:65 + r, slots(g), :].bitcast(F32), part[:, g % 2, :].bitcast(F32)).then_inc(m_in[g % 2], 16)

            sp.wait_ge(r_ready, b * T)
            sp.dma_start(x_rows[:], x[b].rearrange("(t p) h -> p t h", p=P)).then_inc(x_in, 16)
            fill(0)
            fill(1)
            fill(2)
            max_rows(0)
            for n in range(STEPS):
                g, c = divmod(n, T)
                if c == 0 and 0 < g and g + 2 < G:
                    fill(g + 2)
                for item in ahead[n]:
                    if item[0] == "t":
                        max_rows(item[1])
            for t in range(T):
                sp.wait_ge(r_ready, b * T + t + 1)
                sp.dma_start(middle[b, t * P:t * P + P, :], y[:, t, :]).then_inc(rows_out, 16)
        sp.wait_ge(rows_out, B * T * 16)

    @block.gpsimd
    def _(pool):
        pool.memset(ident[:], 0.0).then_inc(const_a, 1)
        pool.wait_ge(const_a, 1)
        pool.affine_select(out=ident[:], in_=ident[:], compare_op=ALU.not_equal, fill=1.0, base=0,
                           pattern=[[-1, P]], channel_multiplier=1).then_inc(const_a, 1)
        pool.memset(minus_half[:], -0.5).then_inc(const_a, 1)
        pool.memset(q_st[:].bitcast(F32), 0.0).then_inc(const_a, 1)
        pool.memset(k_st[:].bitcast(F32), 0.0).then_inc(const_a, 1)
        pool.memset(v_one[:], 1.0).then_inc(const_a, 1)
        pool.wait_ge(const_a, 6)
        pool.memset(k_st[64:66].bitcast(F32), -1.0).then_inc(const_a, 1)

        pool.wait_ge(const_a, 7)

        with pool.Fori(0, B) as b:
            def inverse_std(i):
                pool.wait_ge(ln_aggr, (b * 2 + i + 1) * AGGR)
                pool.tensor_tensor(rstd[:], varpe[:], minus_half[:], ALU.pow).then_inc(ln_rstd, 1)

            def normalise(o):
                pool.wait_ge(den_rec, b * O + o + 1)
                if o == 0:
                    pool.wait_ge(o_ps, b * T)
                pool.tensor_tensor(cT_h[:, o, :], ctx_raw[:], den_inv[:], ALU.mult).then_inc(c_h, 1)
                pool.wait_ge(c_h, b * O + o + 1)
                pool.tensor_tensor(ctx_raw[:], ctx_raw[:], den_inv[:], ALU.mult).then_inc(c_norm, 1)
                pool.wait_ge(c_norm, b * O + o + 1)
                pool.tensor_tensor(cT_l[:, o, :], ctx_raw[:], cT_h[:, o, :].bitcast(F32), ALU.subtract).then_inc(c_l, 1)

            inverse_std(0)
            for n in range(STEPS):
                g, c = divmod(n, T)
                if c == 1 and g % 2 == 0 and g > 0:
                    normalise(g // 2 - 1)
            normalise(O - 1)
            inverse_std(1)
            for t in range(T):
                pool.wait_ge(yn_ready, b * T + t + 1)
                pool.tensor_tensor(y[:, t, :], y[:, t, :], x_rows[:, t, :], ALU.add).then_inc(r_ready, 1)

    @block.scalar
    def _(act):
        act.wait_ge(b_in, 16 * (4 * D + 2))
        act.mul(b_qk[:, 0, :], b_qk[:, 0, :], float(D) ** -0.5).then_inc(w_high, 1)
        for i, n in enumerate("qkvo"):
            if n == "q":
                act.wait_ge(q_scaled, 1)
            else:
                act.wait_ge(w_in[n], 128 if n == "o" else 16)
            for c in range(KC):
                src, dst = probs[:, i % 2, c, :], w_h[n][:, c, :]
                if n in "qk":
                    src = src.rearrange("p (a h d) -> p a d h", h=GH, d=D)
                    dst = dst.rearrange("p (a d h) -> p a d h", h=GH, d=D)
                act.copy(dst, src).then_inc(w_high, 1)

        with act.Fori(0, B) as b:
            def project_high(what, o):
                i = place[(what, o)]
                first = {"q": 0, "k": 2}[what]
                act.wait_ge(rot_full, b * ROT + i + 1)
                for g in ((2 * o - 1, 2 * o - 2) if o else ()):
                    done = len([u for u in range(g + 1) if u % SETS == g % SETS])
                    act.wait_ge(stack_in[g % SETS], (b * fills[g % SETS] + done) * FILL)
                act.activation(qkT[:, first, :], rot[i % 2][:], ACT.Identity,
                               bias=b_qk[:, first // 2, o:o + 1]).then_inc(qk_h, 1)

            def contexts_even(o):
                act.wait_ge(pv_done, b * STEPS + (2 * o + 1) * T)
                act.wait_ge(c_l, b * O + o)
                act.mul(ctx_raw[:], cps[0][:], half_mask[:, 0:1]).then_inc(c0_out, 1)
                act.wait_ge(den_sh, b * O + o)
                act.mul(den[:], cps[0][:], half_mask[:, 1:2]).then_inc(c0_out, 1)

            def invert(o):
                act.wait_ge(den_sh, b * O + o + 1)
                act.activation(den_inv[:], den_inv[:], ACT.Ln).then_inc(den_ln, 1)
                act.wait_ge(den_ln, b * O + o + 1)
                act.activation(den_inv[:], den_inv[:], ACT.Exp, scale=-1.0).then_inc(den_rec, 1)

            for c in range(KC):
                act.wait_ge(xT_ps, b * KC + c + 1)
                if c == 0:
                    act.wait_ge(v_ps, b * T)
                act.copy(xT_h[:, c, :], work[:, c, :]).then_inc(xTh, 1)
            for item in before:
                if item[0] in "qk":
                    project_high(*item)
            for n in range(STEPS):
                g, c = divmod(n, T)
                for item in ahead[n]:
                    if item[0] in "qk":
                        project_high(*item)
                for u in range(2):
                    act.wait_ge(st_full, (b * STEPS + n) * 2 + u + 1)
                    if n >= 2:
                        act.wait_ge(pv_done, b * STEPS + n - 1)
                    if n == 1:
                        act.wait_ge(rows_out, b * T * 16)
                    act.activation(probs[:, n % 2, 2 * u:2 * u + 2, :], work[:, 2 * u:2 * u + 2, :], ACT.Exp).then_inc(p_full, 1)
                if c == 2 and g % 2 == 1:
                    contexts_even(g // 2)
                if c == 1 and g % 2 == 0 and g > 0:
                    invert(g // 2 - 1)
            invert(O - 1)

    @block.vector
    def _(dve):
        dve.wait_ge(const_a, 2)
        dve.tensor_reduce(half_mask[:], ident[:].rearrange("p (j e d) -> p e j d", j=GH, e=2), AX.XY, ALU.add).then_inc(const_v, 1)
        dve.wait_ge(w_in["q"], 16)
        dve.tensor_scalar(probs[:, 0], probs[:, 0], float(D) ** -0.5, None, ALU.mult).then_inc(q_scaled, 1)
        dve.wait_ge(q_scaled, 1)
        for i, n in enumerate("qkvo"):
            dve.wait_ge(w_high, 1 + (i + 1) * KC)
            for c in range(KC):
                src, high, dst = probs[:, i % 2, c, :], w_h[n][:, c, :].bitcast(F32), w_l[n][:, c, :]
                if n in "qk":
                    src = src.rearrange("p (a h d) -> p a d h", h=GH, d=D)
                    high, dst = (a.rearrange("p (a d h) -> p a d h", h=GH, d=D) for a in (high, dst))
                last = dve.tensor_tensor(dst, src, high, ALU.subtract)
            last.then_inc(w_split, 1)

        with dve.Fori(0, B) as b:
            def norm_stats(i, rows):
                for t in range(T):
                    dve.bn_stats(stats[:, t, :], rows[:, t, :]).then_inc(ln_stat, 1)
                aggregate(dve, b * 2 + i, T, H, stats, mean, spread, varpe, ln_stat, ln_aggr)

            def consume(item):
                i = place[item]
                bank = rot[i % 2]
                dve.wait_ge(rot_full, b * ROT + i + 1)
                if item[0] == "s":
                    _, g, j, qc = item
                    dve.tensor_reduce(maxima[:, g % 2, j * T + qc:j * T + qc + 1], bank[:], AX.X, ALU.max).then_inc(rot_free, 1)
                elif item[0] == "t":
                    g = item[1]
                    rows = bank[0:GH * T, 0:P]
                    if g >= 2:
                        dve.wait_ge(m_in[g % 2], (b * (G // 2) + g // 2) * 32)
                    else:
                        dve.wait_ge(m_in[g % 2], b * (G // 2) * 32)
                    dve.tensor_copy(max_h[:, g % 2, :], rows).then_inc(maxh, 1)
                    dve.wait_ge(maxh, b * G + g + 1)
                    dve.tensor_tensor(max_l[:, g % 2, :], rows, max_h[:, g % 2, :].bitcast(F32), ALU.subtract).then_inc(rot_free, 1)
                else:
                    what, o = item
                    first = {"q": 0, "k": 2}[what]
                    dve.wait_ge(qk_h, b * 2 * O + 2 * o + first // 2 + 1)
                    for g in ((2 * o - 1, 2 * o - 2) if o else ()):
                        done = len([u for u in range(g + 1) if u % SETS == g % SETS])
                        dve.wait_ge(stack_in[g % SETS], (b * fills[g % SETS] + done) * FILL)
                    dve.scalar_tensor_tensor(qkT[:, first + 1, :], bank[:], b_qk[:, first // 2, o:o + 1],
                                             qkT[:, first, :].bitcast(F32), ALU.add, ALU.subtract).then_inc(rot_free, 1)

            def contexts_odd(o):
                dve.wait_ge(pv_done, b * STEPS + (2 * o + 2) * T)
                dve.wait_ge(c0_out, (b * O + o + 1) * 2)
                dve.scalar_tensor_tensor(den[:], cps[1][:], half_mask[:, 0:1], den[:], ALU.mult, ALU.add).then_inc(c1_out, 1)
                dve.wait_ge(c1_out, (b * O + o) * 2 + 1)
                dve.wait_ge(c_norm, b * O + o)
                dve.scalar_tensor_tensor(ctx_raw[:], cps[1][:], half_mask[:, 1:2], ctx_raw[:], ALU.mult, ALU.add).then_inc(c1_out, 1)
                dve.stream_shuffle(den_inv[:], den[:], [(i + D) % 32 for i in range(32)]).then_inc(den_sh, 1)

            dve.wait_ge(x_in, b * 16 + 16)
            norm_stats(0, x_rows)
            dve.wait_ge(ln_rstd, b * 2 + 1)
            for t in range(T):
                dve.tensor_scalar(xn[:, t, :], x_rows[:, t, :], mean[:, t:t + 1], rstd[:, t:t + 1],
                                  ALU.subtract, ALU.mult).then_inc(xn_ready, 1)
            for c in range(KC):
                dve.wait_ge(xTh, b * KC + c + 1)
                dve.tensor_tensor(xT_l[:, c, :], work[:, c, :], xT_h[:, c, :].bitcast(F32), ALU.subtract).then_inc(xTl, 1)
            for item in before:
                if item[0] in "qk":
                    consume(item)
            for t in range(T):
                dve.wait_ge(v_ps, b * T + t + 1)
                for e in range(2):
                    dst = v_one[:, t].rearrange("p (a e j) w -> p e a j w", e=2, j=GH)[:, e, :, :, e * D:e * D + D]
                    src, bias = (a.rearrange("p (a e j d) -> p e a j d", e=2, j=GH, d=D)[:, e] for a in (work[:, t, :], bv_rows[:]))
                    dve.tensor_tensor(dst, src, bias, ALU.add).then_inc(v_ready, 1)
            for item in before:
                if item[0] not in "qk":
                    consume(item)
            for n in range(STEPS):
                g, c = divmod(n, T)
                for item in ahead[n]:
                    consume(item)
                if c == 1 and g % 2 == 0 and g > 0:
                    contexts_odd(g // 2 - 1)
            contexts_odd(O - 1)
            for t in range(T):
                dve.wait_ge(o_ps, b * T + t + 1)
                dve.tensor_tensor(y[:, t, :], work[:, t, :], bo_rows[:], ALU.add).then_inc(y_ready, 1)
            dve.wait_ge(y_ready, b * T + T)
            norm_stats(1, y)
            dve.wait_ge(ln_rstd, b * 2 + 2)
            for t in range(T):
                dve.tensor_scalar(y[:, t, :], y[:, t, :], mean[:, t:t + 1], rstd[:, t:t + 1],
                                  ALU.subtract, ALU.mult).then_inc(yn_ready, 1)

    @block.tensor
    def _(pe):
        pe.wait_ge(const_a, 7)
        pe.wait_ge(w_split, 4)

        def product(out, left, right, first, last):
            for i, (a, c) in enumerate(((0, 0), (1, 0), (0, 1))):
                mm = pe.matmul(out, left[a], right[c], start=first and i == 0, stop=last and i == 2)
            return mm

        with pe.Fori(0, B) as b:
            def item_products(item):
                i = place[item]
                bank = rot[i % 2]
                pe.wait_ge(rot_free, b * ROT + i - 1 if i >= 2 else b * ROT)
                if item[0] == "s":
                    _, g, j, qc = item
                    if qc == 0 and j == 0:
                        done = len([u for u in range(g + 1) if u % SETS == g % SETS])
                        pe.wait_ge(stack_in[g % SETS], (b * fills[g % SETS] + done) * FILL)
                    s = (g % SETS) * GH + j
                    mm = pe.matmul(bank[:], q_st[:, s, qc * P:qc * P + P], k_st[:, s, :], start=True, stop=True)
                elif item[0] == "t":
                    g = item[1]
                    pe.wait_ge(rot_free, b * ROT + place[("s", g, GH - 1, T - 1)] + 1)
                    mm = pe.transpose(bank[0:GH * T, 0:P], maxima[:, g % 2, :], ident[:])
                else:
                    what, o = item
                    for c in range(KC):
                        cols = slice(o * P, o * P + P)
                        mm = product(bank[:], (w_h[what][:, c, cols], w_l[what][:, c, cols]),
                                     (xT_h[:, c, :], xT_l[:, c, :]), c == 0, c == KC - 1)
                mm.then_inc(rot_full, 1)

            def scores(n, u):
                g, c = divmod(n, T)
                if n:
                    pe.wait_ge(p_full, (b * STEPS + n) * 2 + u - 1)
                if c == 0 and u == 0:
                    pe.wait_ge(m_in[g % 2], (b * (G // 2) + g // 2 + 1) * 32)
                for j in range(2 * u, 2 * u + 2):
                    s = (g % SETS) * GH + j
                    mm = pe.matmul(work[:, j, :], k_st[:, s, c * P:c * P + P], q_st[:, s, :], start=True, stop=True)
                mm.then_inc(st_full, 1)

            def contexts(n):
                g, c = divmod(n, T)
                pe.wait_ge(p_full, (b * STEPS + n + 1) * 2)
                if c == 0:
                    pe.wait_ge(c1_out if g % 2 else c0_out, (b * O + g // 2) * 2)
                for j in range(GH):
                    mm = pe.matmul(cps[g % 2][32 * j:32 * j + 32, :], v_one[:, c, GH * g + j, :],
                                   probs[:, n % 2, j, :], start=(c == 0), stop=(c == T - 1))
                mm.then_inc(pv_done, 1)

            pe.wait_ge(y_ready, b * T)
            for t in range(T):
                pe.wait_ge(xn_ready, b * T + t + 1)
            for c in range(KC):
                for t in range(T):
                    mm = pe.transpose(work[:, c, t * P:t * P + P], xn[:, t, c * P:c * P + P], ident[:])
                mm.then_inc(xT_ps, 1)
            pe.wait_ge(xTl, b * KC + KC)
            for item in before:
                if item[0] in "qk":
                    item_products(item)
            for t in range(T):
                toks = slice(t * P, t * P + P)
                for c in range(KC):
                    mm = product(work[:, t, :], (xT_h[:, c, toks], xT_l[:, c, toks]),
                                 (w_h["v"][:, c, :], w_l["v"][:, c, :]), c == 0, c == KC - 1)
                mm.then_inc(v_ps, 1)
            for item in before:
                if item[0] not in "qk":
                    item_products(item)
            pe.wait_ge(v_ready, (b * T + T) * 2)
            for n in range(STEPS):
                items = ahead[n]
                cut = [len(items) * k // 4 for k in range(5)]
                parts = [items[cut[k]:cut[k + 1]] for k in range(4)]
                for item in parts[0]:
                    item_products(item)
                scores(n, 0)
                for item in parts[1]:
                    item_products(item)
                scores(n, 1)
                for item in parts[2]:
                    item_products(item)
                if n:
                    contexts(n - 1)
                for item in parts[3]:
                    item_products(item)
            contexts(STEPS - 1)
            for o in range(O):
                pe.wait_ge(c_l, b * O + o + 1)
                if o == 0:
                    pe.wait_ge(p_full, (b * STEPS + STEPS) * 2)
                for t in range(T):
                    toks = slice(t * P, t * P + P)
                    mm = product(work[:, t, :], (cT_h[:, o, toks], cT_l[:, o, toks]),
                                 (w_h["o"][:, o, :], w_l["o"][:, o, :]), o == 0, o == O - 1)
                    if o == O - 1:
                        mm.then_inc(o_ps, 1)


def ffn_pass(nc, ctx, ident, middle, gate_w, up_w, down_w, gate_s, up_s, down_s, out):
    B, S, H = middle.shape
    I = gate_w.shape[1]
    T = S // P
    KC = H // P
    F = I // P
    XS = 1024.0
    QN = I // H
    CHUNKS = 2 * KC * QN + F

    sb = lambda name, shape, dt=F32: ctx.enter_context(nc.sbuf_tensor(name, shape, dt))
    ps = lambda name, shape: ctx.enter_context(nc.psum_tensor(name, shape, F32))
    sem = lambda name: ctx.enter_context(nc.semaphore(name))

    gate_q = sb("gate_q", [P, KC, I], F16)
    up_q = sb("up_q", [P, KC, I], F16)
    down_q = sb("down_q", [P, F, H], F32R)
    gs = sb("gate_scale", [P, F])
    us = sb("up_scale", [P, F])
    gs0 = sb("gate_scale_in", [P, F])
    us0 = sb("up_scale_in", [P, F])
    ds_rows = sb("down_scale_rows", [P, H])
    minus_half = sb("minus_half2", [P, T])
    w_raw = sb("w_raw", [P, 4, H])
    w_mag = sb("w_mag", [P, 2, H])
    w_sum = sb("w_sum", [P, 2, H])
    w_rnd = sb("w_rnd", [P, 2, H])
    w_big = sb("w_big", [P, 2, H])

    x_rows = sb("x_rows2", [P, 2, T, H])
    xn = sb("xn2", [P, T, H])
    xT_h = sb("xT2_high", [P, KC, S], F16)
    xT_l = sb("xT2_low", [P, KC, S], F16)
    gate = sb("gate", [P, 2, S])
    fuse = sb("fuse", [P, 2, S])
    fuse_h = sb("fuse_high", [P, 2, S], F32R)
    fuse_l = sb("fuse_low", [P, 2, S], F32R)
    y = sb("y2", [P, T, H])
    stats = sb("stats2", [P, T, 6])
    mean = sb("mean2", [P, T])
    spread = sb("spread2", [P, 3, T])
    varpe = sb("var_plus_eps2", [P, T])
    rstd = sb("rstd2", [P, T])

    gu = ps("gate_up", [P, 2, 2, S])
    acc = ps("down_acc", [P, T, H])

    wr_in = [sem(f"w_raw_in{i}") for i in range(4)]
    s_in = sem("scales_in")
    mag = sem("w_exponent")
    magic = sem("w_magic")
    summed = sem("w_summed")
    rounded = sem("w_rounded")
    big = sem("w_overflow")
    quant = sem("w_quantised")
    s_ready = sem("scales_ready")
    const_p = sem("const2_made")
    x_in = [sem(f"x2_in{i}") for i in range(2)]
    ln_stat = sem("ln2_stat")
    ln_aggr = sem("ln2_aggr")
    ln_rstd = sem("ln2_rstd")
    xn_ready = sem("xn2_ready")
    xT_ps = sem("xT2_in_psum")
    xTh = sem("xT2_high_ready")
    xTl = sem("xT2_low_ready")
    gu_ps = sem("gate_up_in_psum")
    silu = sem("gate_ready")
    fused = sem("fuse_ready")
    fh = sem("fuse_high_ready")
    fl = sem("fuse_low_ready")
    down_done = sem("down_done")
    y_ready = sem("y2_ready")
    yn_ready = sem("y2_normalised")
    r_ready = sem("row_sum2_ready")
    rows_out = sem("rows2_out")

    jobs = []
    for c in range(KC):
        for q in range(QN):
            jobs.append((gate_w[c * P:c * P + P, q * H:q * H + H], gate_q[:, c, q * H:q * H + H]))
            jobs.append((up_w[c * P:c * P + P, q * H:q * H + H], up_q[:, c, q * H:q * H + H]))
    for f in range(F):
        jobs.append((down_w[f * P:f * P + P, :], down_q[:, f, :]))
    assert len(jobs) == CHUNKS

    block = ctx.enter_context(nc.Block())

    @block.sync
    def _(sp):
        sp.dma_start(gs0[:], gate_s.rearrange("(f p) -> p f", p=P), allow_slow_non_contiguous=True).then_inc(s_in, 16)
        sp.dma_start(us0[:], up_s.rearrange("(f p) -> p f", p=P), allow_slow_non_contiguous=True).then_inc(s_in, 16)
        sp.dma_start(ds_rows[:], down_s.partition_broadcast(P)).then_inc(s_in, 16)
        for i, (src, _) in enumerate(jobs):
            if i >= 4:
                sp.wait_ge(summed, i - 3)
            sp.dma_start(w_raw[:, i % 4, :], src).then_inc(wr_in[i % 4], 16)
        sp.dma_start(x_rows[:, 0], middle[0].rearrange("(t p) h -> p t h", p=P)).then_inc(x_in[0], 16)
        with sp.Fori(0, B // 2) as pair:
            for k in range(2):
                b = pair * 2 + k
                if k == 0:
                    sp.wait_ge(r_ready, b * T)
                    sp.dma_start(x_rows[:, 1], middle[b + 1].rearrange("(t p) h -> p t h", p=P)).then_inc(x_in[1], 16)
                for t in range(T):
                    sp.wait_ge(r_ready, b * T + t + 1)
                    sp.dma_start(out[b, t * P:t * P + P, :], y[:, t, :]).then_inc(rows_out, 16)
                if k == 1:
                    sp.dma_start(x_rows[:, 0], middle[(pair * 2 + 2) % B].rearrange("(t p) h -> p t h", p=P)).then_inc(x_in[0], 16)
        sp.wait_ge(rows_out, B * T * 16)
        sp.wait_ge(x_in[0], (B // 2 + 1) * 16)

    @block.gpsimd
    def _(pool):
        pool.memset(minus_half[:], -0.5).then_inc(const_p, 1)
        for i in range(CHUNKS):
            pool.wait_ge(magic, i + 1)
            pool.wait_ge(wr_in[i % 4], (i // 4 + 1) * 16)
            if i >= 2:
                pool.wait_ge(rounded, i - 1)
            pool.tensor_tensor(w_sum[:, i % 2, :], w_raw[:, i % 4, :], w_mag[:, i % 2, :], ALU.add).then_inc(summed, 1)
            pool.wait_ge(summed, i + 1)
            if i >= 2:
                pool.wait_ge(quant, i - 1)
            pool.tensor_tensor(w_rnd[:, i % 2, :], w_sum[:, i % 2, :], w_mag[:, i % 2, :], ALU.subtract).then_inc(rounded, 1)
        pool.wait_ge(const_p, 1)

        with pool.Fori(0, B) as b:
            def inverse_std(i):
                pool.wait_ge(ln_aggr, (b * 2 + i + 1) * AGGR)
                pool.tensor_tensor(rstd[:], varpe[:], minus_half[:], ALU.pow).then_inc(ln_rstd, 1)

            inverse_std(0)
            for f in range(F):
                n = b * F + f
                pool.wait_ge(fh, n + 1)
                pool.wait_ge(down_done, n - 1 if f >= 2 else b * F)
                pool.tensor_tensor(fuse_l[:, f % 2, :], fuse[:, f % 2, :], fuse_h[:, f % 2, :].bitcast(F32), ALU.subtract).then_inc(fl, 1)
            inverse_std(1)

    @block.scalar
    def _(act):
        for i in range(CHUNKS):
            act.wait_ge(rounded, i + 1)
            if i >= 2:
                act.wait_ge(quant, i - 1)
            act.mul(w_big[:, i % 2, :], w_rnd[:, i % 2, :], 1.1 * 2.0 ** 119).then_inc(big, 1)
        with act.Fori(0, B) as b:
            for c in range(KC):
                act.wait_ge(xT_ps, b * KC + c + 1)
                if c == 0:
                    act.wait_ge(gu_ps, b * 2 * F)
                act.mul(xT_h[:, c, :], gu[:, c // 2, c % 2, :], XS).then_inc(xTh, 1)
            for f in range(F):
                act.wait_ge(gu_ps, (b * F + f) * 2 + 1)
                act.wait_ge(fused, b * F + f - 1 if f >= 2 else b * F)
                act.activation(gate[:, f % 2, :], gu[:, f % 2, 0, :], ACT.Silu, scale=gs[:, f:f + 1]).then_inc(silu, 1)
                act.wait_ge(fused, b * F + f + 1)
                act.wait_ge(down_done, b * F + f - 1 if f >= 2 else b * F)
                act.copy(fuse_h[:, f % 2, :], fuse[:, f % 2, :]).then_inc(fh, 1)

    @block.vector
    def _(dve):
        dve.wait_ge(s_in, 48)
        dve.tensor_scalar(gs[:], gs0[:], 1.0 / XS, None, ALU.mult).then_inc(s_ready, 1)
        dve.tensor_scalar(us[:], us0[:], 1.0 / XS, None, ALU.mult).then_inc(s_ready, 1)

        def magic_number(i):
            dve.wait_ge(wr_in[i % 4], (i // 4 + 1) * 16)
            if i >= 2:
                dve.wait_ge(rounded, i - 1)
            dve.tensor_scalar(w_mag[:, i % 2, :].bitcast(I32), w_raw[:, i % 4, :].bitcast(I32), 0x7F800000, None, ALU.bitwise_and).then_inc(mag, 1)
            dve.wait_ge(mag, i + 1)
            dve.tensor_scalar(w_mag[:, i % 2, :], w_mag[:, i % 2, :], 2.0 ** -6, 1.5 * 2.0 ** 20, ALU.max, ALU.mult).then_inc(magic, 1)

        def store(i):
            dve.wait_ge(big, i + 1)
            dve.scalar_tensor_tensor(jobs[i][1], w_big[:, i % 2, :], 0.0, w_rnd[:, i % 2, :], ALU.mult, ALU.add).then_inc(quant, 1)

        for i in range(CHUNKS):
            magic_number(i)
            if i >= 2:
                store(i - 2)
        store(CHUNKS - 2)
        store(CHUNKS - 1)

        with dve.Fori(0, B // 2) as pair:
            for k in range(2):
                b = pair * 2 + k

                def norm_stats(i, rows):
                    for t in range(T):
                        dve.bn_stats(stats[:, t, :], rows[:, t, :]).then_inc(ln_stat, 1)
                    aggregate(dve, b * 2 + i, T, H, stats, mean, spread, varpe, ln_stat, ln_aggr)

                dve.wait_ge(x_in[k], pair * 16 + 16)
                norm_stats(0, x_rows[:, k])
                dve.wait_ge(ln_rstd, b * 2 + 1)
                for t in range(T):
                    dve.tensor_scalar(xn[:, t, :], x_rows[:, k, t, :], mean[:, t:t + 1], rstd[:, t:t + 1],
                                      ALU.subtract, ALU.mult).then_inc(xn_ready, 1)
                for c in range(KC):
                    dve.wait_ge(xTh, b * KC + c + 1)
                    dve.scalar_tensor_tensor(xT_l[:, c, :], gu[:, c // 2, c % 2, :], XS, xT_h[:, c, :],
                                             ALU.mult, ALU.subtract).then_inc(xTl, 1)
                for f in range(F):
                    dve.wait_ge(gu_ps, (b * F + f) * 2 + 2)
                    dve.wait_ge(silu, b * F + f + 1)
                    if f >= 2:
                        dve.wait_ge(fl, b * F + f - 1)
                    dve.scalar_tensor_tensor(fuse[:, f % 2, :], gu[:, f % 2, 1, :], us[:, f:f + 1], gate[:, f % 2, :],
                                             ALU.mult, ALU.mult).then_inc(fused, 1)
                dve.wait_ge(rows_out, b * T * 16)
                dve.wait_ge(down_done, b * F + F)
                for t in range(T):
                    dve.tensor_tensor(y[:, t, :], acc[:, t, :], ds_rows[:], ALU.mult).then_inc(y_ready, 1)
                dve.wait_ge(y_ready, b * T + T)
                norm_stats(1, y)
                dve.wait_ge(ln_rstd, b * 2 + 2)
                for t in range(T):
                    dve.tensor_scalar(y[:, t, :], y[:, t, :], mean[:, t:t + 1], rstd[:, t:t + 1],
                                      ALU.subtract, ALU.mult).then_inc(yn_ready, 1)
                for t in range(T):
                    dve.wait_ge(yn_ready, b * T + t + 1)
                    dve.tensor_tensor(y[:, t, :], y[:, t, :], x_rows[:, k, t, :], ALU.add).then_inc(r_ready, 1)

    @block.tensor
    def _(pe):
        pe.wait_ge(quant, CHUNKS)
        pe.wait_ge(s_ready, 2)
        with pe.Fori(0, B) as b:
            def down(f):
                pe.wait_ge(fl, b * F + f + 1)
                if f == 0:
                    pe.wait_ge(y_ready, b * T)
                for t in range(T):
                    toks = slice(t * P, t * P + P)
                    for i, part in enumerate((fuse_h, fuse_l)):
                        mm = pe.matmul(acc[:, t, :], part[:, f % 2, toks], down_q[:, f, :],
                                       start=(f == 0 and i == 0), stop=(f == F - 1 and i == 1))
                mm.then_inc(down_done, 1)

            for t in range(T):
                pe.wait_ge(xn_ready, b * T + t + 1)
            pe.wait_ge(fused, b * F)
            for c in range(KC):
                for t in range(T):
                    mm = pe.transpose(gu[:, c // 2, c % 2, t * P:t * P + P], xn[:, t, c * P:c * P + P], ident[:])
                mm.then_inc(xT_ps, 1)
            pe.wait_ge(xTl, b * KC + KC)
            for f in range(F):
                if f >= 2:
                    pe.wait_ge(fused, b * F + f - 1)
                for w, weight in enumerate((gate_q, up_q)):
                    for c in range(KC):
                        for i, part in enumerate((xT_h, xT_l)):
                            mm = pe.matmul(gu[:, f % 2, w, :], weight[:, c, f * P:f * P + P], part[:, c, :],
                                           start=(c == 0 and i == 0), stop=(c == KC - 1 and i == 1))
                    mm.then_inc(gu_ps, 1)
                if f:
                    down(f - 1)
            down(F - 1)


_INS = ['L0_attn_hidden_states', 'L0_attn_Wq', 'L0_attn_bq', 'L0_attn_Wk', 'L0_attn_bk', 'L0_attn_Wv', 'L0_attn_bv',
        'L0_attn_Wo', 'L0_attn_bo', 'L0_ffn_gate_w', 'L0_ffn_up_w', 'L0_ffn_down_w', 'L0_ffn_gate_scale',
        'L0_ffn_up_scale', 'L0_ffn_down_scale']


def kernel(**inputs):
    import numpy as np
    import concourse.bacc as bacc
    from concourse.bass_utils import run_bass_kernel_spmd

    nc = bacc.Bacc("TRN2", target_bir_lowering=False, num_devices=1)
    arrays, args = {}, []
    for name in _INS:
        a = np.ascontiguousarray(inputs[name])
        arrays[f"in_{name}"] = a
        args.append(nc.dram_tensor(f"in_{name}", a.shape, mybir.dt.from_np(a.dtype), kind="ExternalInput").ap())
    shape = inputs[_INS[0]].shape
    out = nc.dram_tensor("out_rows", shape, F32, kind="ExternalOutput").ap()
    layer(nc, *args, out)
    r = run_bass_kernel_spmd(nc, [arrays], core_ids=[0])
    return r.results[0]["out_rows"]
```

```python
from contextlib import ExitStack

import concourse.bass as bass
from concourse import mybir

F32 = mybir.dt.float32
F32R = mybir.dt.float32r
F16 = mybir.dt.float16
BF16 = mybir.dt.bfloat16
I32 = mybir.dt.int32
ALU = mybir.AluOpType
ACT = mybir.ActivationFunctionType
AX = mybir.AxisListType

P = 128
NH = 32
D = 16
GH = 4
EPS = 1e-5
SETS = 4
FILL = 13 * 16
LEAD = 7


IDENT, STACKS_CLEAR, ONES, CONSTS = 2, 6, 7, 11
PRODUCTS = ((0, 0), (0, 1), (0, 2), (1, 0), (1, 1), (2, 0))
AGGR = 7


def aggregate(dve, n, T, width, stats, mean, spread, varpe, stat_done, step_done):
    dve.wait_ge(stat_done, n * T + T)
    dve.tensor_tensor(spread[:, 0, :], stats[:, :, 1], stats[:, :, 4], ALU.add).then_inc(step_done, 1)
    dve.tensor_tensor(spread[:, 1, :], stats[:, :, 1], stats[:, :, 4], ALU.subtract).then_inc(step_done, 1)
    dve.tensor_tensor(spread[:, 2, :], stats[:, :, 2], stats[:, :, 5], ALU.add).then_inc(step_done, 1)
    dve.wait_ge(step_done, n * AGGR + 2)
    dve.tensor_scalar(mean[:], spread[:, 0, :], 0.5, None, ALU.mult).then_inc(step_done, 1)
    dve.tensor_tensor(varpe[:], spread[:, 1, :], spread[:, 1, :], ALU.mult).then_inc(step_done, 1)
    dve.wait_ge(step_done, n * AGGR + 5)
    dve.scalar_tensor_tensor(varpe[:], varpe[:], width / 4.0, spread[:, 2, :], ALU.mult, ALU.add).then_inc(step_done, 1)
    dve.wait_ge(step_done, n * AGGR + 6)
    dve.tensor_scalar(varpe[:], varpe[:], 1.0 / width, EPS, ALU.mult, ALU.add).then_inc(step_done, 1)


def layer(nc, x, Wq, bq, Wk, bk, Wv, bv, Wo, bo, gate_w, up_w, down_w, gate_s, up_s, down_s, out):
    with ExitStack() as ctx:
        B, S, H = x.shape
        middle = nc.dram_tensor("middle_rows", [B + 1, S, H], F32, kind="Internal").ap()
        ident = ctx.enter_context(nc.sbuf_tensor("ident", [P, P], F32))
        with nc.Block() as block:
            shared = attention_pass(nc, ctx, block, ident, x, Wq, bq, Wk, bk, Wv, bv, Wo, bo,
                                    (gate_w, up_w, down_w), middle)
            ffn_pass(nc, ctx, block, shared, ident, middle, gate_s, up_s, down_s, out)


class Shared:
    pass


def weight_rounding(nc, ctx, gate_w, up_w, down_w):
    H, I = gate_w.shape
    KC = H // P
    F = I // P
    QF = H // P
    RAW = 8

    sb = lambda name, shape, dt=F32: ctx.enter_context(nc.sbuf_tensor(name, shape, dt))
    sem = lambda name: ctx.enter_context(nc.semaphore(name))

    gate_q = sb("gate_q", [P, KC, I], F16)
    up_q = sb("up_q", [P, KC, I], F16)
    down_q = sb("down_q", [P, F, H], F32R)
    w_raw = sb("w_raw", [P, RAW, H])
    w_magic = sb("w_magic", [P, 2, H])
    w_sum = sb("w_sum", [P, 2, H])
    w_round = sb("w_rounded", [P, 2, H])
    w_big = sb("w_overflow", [P, 2, H])

    raw_in = [sem(f"w_raw_in{i}") for i in range(RAW)]
    power = sem("w_power_ready")
    magic = sem("w_magic_ready")
    summed = sem("w_summed")
    rounded = sem("w_rounded_ready")
    big = sem("w_overflow_ready")
    quant = sem("w_quantised")

    jobs, gate_up_jobs, down_job = [], {}, {}
    for q in range(F // QF):
        cols = slice(q * H, q * H + H)
        for c in range(KC):
            jobs.append((gate_w[c * P:c * P + P, cols], gate_q[:, c, cols]))
            jobs.append((up_w[c * P:c * P + P, cols], up_q[:, c, cols]))
        gate_up_jobs[q] = len(jobs)
        for f in range(q * QF, q * QF + QF):
            jobs.append((down_w[f * P:f * P + P, :], down_q[:, f, :]))
            down_job[f] = len(jobs)

    def load(sp, i):
        if i >= RAW:
            sp.wait_ge(summed, i - RAW + 1)
        sp.dma_start(w_raw[:, i % RAW, :], jobs[i][0]).then_inc(raw_in[i % RAW], 16)

    def add_magic(dve, i):
        dve.wait_ge(raw_in[i % RAW], (i // RAW + 1) * 16)
        if i >= 2:
            dve.wait_ge(rounded, i - 1)
        w, m = w_raw[:, i % RAW, :], w_magic[:, i % 2, :]
        dve.tensor_scalar(m.bitcast(I32), w.bitcast(I32), 0x7F800000, None, ALU.bitwise_and).then_inc(power, 1)
        dve.wait_ge(power, i + 1)
        dve.tensor_scalar(m, m, 2.0 ** -6, 1.5 * 2.0 ** 20, ALU.max, ALU.mult).then_inc(magic, 1)
        dve.wait_ge(magic, i + 1)
        dve.tensor_tensor(w_sum[:, i % 2, :], w, m, ALU.add).then_inc(summed, 1)

    def take_magic(pool, i):
        pool.wait_ge(summed, i + 1)
        if i >= 2:
            pool.wait_ge(quant, i - 1)
        pool.tensor_tensor(w_round[:, i % 2, :], w_sum[:, i % 2, :], w_magic[:, i % 2, :], ALU.subtract).then_inc(rounded, 1)

    def overflow(act, i):
        act.wait_ge(rounded, i + 1)
        if i >= 2:
            act.wait_ge(quant, i - 1)
        act.mul(w_big[:, i % 2, :], w_round[:, i % 2, :], 1.1 * 2.0 ** 119).then_inc(big, 1)

    def store(dve, i):
        dve.wait_ge(big, i + 1)
        dve.scalar_tensor_tensor(jobs[i][1], w_big[:, i % 2, :], 0.0, w_round[:, i % 2, :], ALU.mult, ALU.add).then_inc(quant, 1)

    def quantise(dve, i):
        add_magic(dve, i)
        if i >= 1:
            store(dve, i - 1)
        if i == len(jobs) - 1:
            store(dve, i)

    r = Shared()
    r.F, r.QF, r.count, r.gate_up_jobs, r.down_job = F, QF, len(jobs), gate_up_jobs, down_job
    r.quant, r.gate_q, r.up_q, r.down_q = quant, gate_q, up_q, down_q
    r.load, r.quantise, r.take_magic, r.overflow = load, quantise, take_magic, overflow
    return r


def attention_pass(nc, ctx, block, ident, x, Wq, bq, Wk, bk, Wv, bv, Wo, bo, ffn_weights, middle):
    B, S, H = x.shape
    T = S // P
    KC = H // P
    G = NH // GH
    O = G // 2
    STEPS = G * T

    turns = ExitStack()
    sb = lambda name, shape, dt=F32: turns.enter_context(nc.sbuf_tensor(name, shape, dt))
    keep = lambda name, shape, dt=F32: ctx.enter_context(nc.sbuf_tensor(name, shape, dt, side="right"))
    ps = lambda name, shape: turns.enter_context(nc.psum_tensor(name, shape, F32))
    sem = lambda name: ctx.enter_context(nc.semaphore(name))

    w_h = {n: (keep if n == "o" else sb)(f"w{n}_high", [P, KC, H], F32R) for n in "qkvo"}
    w_l = {n: (keep if n == "o" else sb)(f"w{n}_low", [P, KC, H], F32R) for n in "qkvo"}
    b_qk = keep("bias_qk", [P, 2, O])
    bv_rows = sb("bias_v_rows", [P, H])
    bo_rows = keep("bias_o_rows", [P, H])
    half_mask = keep("half_mask", [P, 2])
    minus_half = keep("minus_half", [P, T])

    x_rows = sb("x_rows", [P, T, H])
    x_res = keep("x_residual", [P, 2, H])
    y = keep("y", [P, T, H])
    xT_h = sb("xT_high", [P, KC, S], F32R)
    xT_l = sb("xT_low", [P, KC, S], F32R)
    qkT = sb("qkT", [P, 6, S], BF16)
    qk_rest = sb("qk_rest", [P, S])
    v_one = sb("v_one", [P, T, NH, 2 * D])
    q_st = sb("q_stack", [P, SETS * GH, S], BF16)
    k_st = sb("k_stack", [P, SETS * GH, S], BF16)
    probs = sb("probs", [P, 2, GH, S])
    cT_h = keep("ctxT_high", [P, O, S], F32R)
    cT_l = keep("ctxT_low", [P, O, S], F32R)
    ctx_raw = keep("ctx_raw", [P, S])
    den = keep("denominators", [P, S])
    maxima = sb("maxima", [P, 2, GH * T])
    max_part = sb("max_parts", [GH * T, 2, 3, P], BF16)
    max_rest = sb("max_rest", [GH * T, P])
    norms = {n: {k: keep(f"{k}_{n}", s) for k, s in (("stats", [P, T, 6]), ("mean", [P, T]), ("spread", [P, 3, T]),
                                                   ("varpe", [P, T]), ("rstd", [P, T]))} for n in ("in", "out")}

    rot = [ps(f"maxima_scores{i}", [P, S]) for i in range(2)]
    work = ps("scores", [P, 4, S])
    cps = ps("contexts", [P, S])
    side = ps("side", [P, S])

    w_in = {n: sem(f"w{n}_in") for n in "qkvo"}
    b_in = sem("biases_in")
    w_split = sem("w_split")
    w_high = sem("w_high")
    b_scaled = sem("bias_q_scaled")
    q_scaled = sem("q_weight_scaled")
    const_a = sem("constants_made")
    const_v = sem("masks_made")
    x_in = sem("x_in")
    res_in = [sem(f"x_residual_in{i}") for i in range(2)]
    ln_stat = {n: sem(f"ln_{n}_stat") for n in ("in", "out")}
    ln_step = {n: sem(f"ln_{n}_step") for n in ("in", "out")}
    ln_rstd = {n: sem(f"ln_{n}_rstd") for n in ("in", "out")}
    xn_ready = sem("xn_ready")
    side_full = sem("side_full")
    side_free = sem("side_free")
    xTh = sem("xT_high_ready")
    v_half = sem("v_half_copied")
    rot_full = sem("rot_full")
    rot_free = sem("rot_free")
    qk_h = sem("qk_high_ready")
    qk_m = sem("qk_middle_ready")
    qk_l = sem("qk_low_ready")
    stack_in = [sem(f"stack_in{i}") for i in range(SETS)]
    max_step = sem("max_part_ready")
    max_ready = sem("max_parts_ready")
    m_in = [sem(f"max_rows_in{i}") for i in range(2)]
    st_full = sem("scores_full")
    p_full = sem("probs_ready")
    pv_done = sem("contexts_added")
    c0_out = sem("even_contexts_read")
    c1_out = sem("odd_contexts_read")
    den_sh = sem("denominators_shuffled")
    den_ln = sem("denominators_ln")
    den_rec = sem("denominators_inverted")
    c_h = sem("ctx_high_ready")
    c_norm = sem("ctx_normalised")
    c_l = sem("ctx_low_ready")
    yn_ready = sem("y_normalised")
    r_ready = sem("row_sum_ready")
    rows_out = sem("rows_out")

    PROBS0, PV0, ODD0, SHUF0, OUT0 = 2, 2, 1, 1, 16

    def unit(h):
        return [("t", h // GH - 1)] * (h % GH == 0 and h > 0) + [("s", h // GH, h % GH, qc) for qc in range(T)] * (h < NH)

    rot_items = [item for h in range(NH + 1) for item in unit(h)]
    rot_at = {item: i for i, item in enumerate(rot_items)}
    ROT = len(rot_items)
    assert ROT % 2 == 0

    def rot_step(n):
        h = n + LEAD
        if h < NH:
            return [(i, 0) for i in unit(h)]
        return [(("t", G - 1), 0)] * (h == NH) + [(i, 1) for i in unit(h - NH)]

    ahead = [("x", t) for t in range(T)] + [("q", 0), ("k", 0), ("q", 1), ("k", 1), ("v", 0), ("v", 1), ("v", 2)]
    side_steps = {0: ("v", 3), 3: ("q", 2), 4: ("k", 2), 5: ("o", 0), 6: ("o", 1), 7: ("o", 2), 8: ("o", 3),
                  11: ("q", 3), 12: ("k", 3), 14: ("x", 0), 15: ("x", 1), 16: ("x", 2), 17: ("x", 3),
                  19: ("q", 0), 20: ("k", 0), 27: ("q", 1), 28: ("k", 1), 29: ("v", 0), 30: ("v", 1), 31: ("v", 2)}
    side_items = ahead + [i for n, i in sorted(side_steps.items()) if i not in ahead]
    side_at = {item: i for i, item in enumerate(side_items)}
    SIDE = len(side_items)

    start = ([("x", t) for t in range(T)] + [("q", 0), ("k", 0), ("w", "o"), ("v", 0), ("v", 1), ("v", 2)]
             + [("r", h) for h in range(GH + 1)] + [("q", 1), ("k", 1)] + [("r", h) for h in range(GH + 1, LEAD)])
    start_at = {item: i for i, item in enumerate(item for item in start if item[0] not in "rw")}
    assert len(start_at) == len(ahead) and all(start_at[item] <= side_at[item] for item in ahead if item[0] == "v")

    def of_next(item, n):
        return 1 if item in ahead and n >= 14 else 0

    fill_steps = {(4 * g - 11) % STEPS: g for g in range(G)}

    def filled(n, g):
        return (n * (G // SETS) + g // SETS + 1) * FILL

    def slots(g):
        s = g % SETS
        return slice(s * GH, s * GH + GH)

    turns.close()
    rounding = weight_rounding(nc, ctx, *ffn_weights)
    BEFORE = 3
    BESIDE = BEFORE + T + 1
    shared = Shared()
    shared.rounding, shared.rounded, shared.minus_half = rounding, BESIDE, minus_half
    shared.side_free, shared.side_items = side_free, B * SIDE + len(ahead) + T
    shared.rows_out, shared.rows_before_last = rows_out, OUT0 + B * T * 16

    @block.sync
    def _(sp):
        def load_weight(n, W, slot):
            dst = probs[:, slot]
            if n == "o":
                v = W.rearrange("(o e j d) n -> j e d o n", o=O, e=2, j=GH)
                for j in range(GH):
                    for e in range(2):
                        lo = 32 * j + D * e
                        sp.dma_start(dst[lo:lo + D, :, :], v[j, e]).then_inc(w_in[n], 16)
            else:
                sp.dma_start(dst, W.rearrange("(c p) n -> p c n", p=P)).then_inc(w_in[n], 16)

        def load_x(n):
            sp.dma_start(x_rows[:], x[n % B].rearrange("(t p) h -> p t h", p=P)).then_inc(x_in, 16)

        load_weight("q", Wq, 0)
        load_weight("k", Wk, 1)
        load_x(0)
        for i, bias in enumerate((bq, bk)):
            v = bias.rearrange("(o g h d) -> g h d o", o=O, g=2, h=GH)
            for g in range(2):
                for h in range(GH):
                    rows = slice(64 * g + h, 64 * g + 64, GH)
                    sp.dma_start(b_qk[rows, i, :], v[g, h], allow_slow_non_contiguous=True).then_inc(b_in, 16)
        sp.dma_start(bv_rows[:], bv.partition_broadcast(P)).then_inc(b_in, 16)
        sp.dma_start(bo_rows[:], bo.partition_broadcast(P)).then_inc(b_in, 16)
        sp.wait_ge(w_split, 1)
        load_weight("v", Wv, 0)
        sp.wait_ge(w_split, 2)
        load_weight("o", Wo, 1)

        def fill(n, g):
            half = slice(64 * (g % 2), 64 * (g % 2) + 64)
            sp.wait_ge(qk_l, (n * O + g // 2) * 2 + 2)
            sp.dma_start(q_st[96:99, slots(g), :], k_st[112:115, slots(g), :]).then_inc(stack_in[g % SETS], 16)
            for r, (qp, kp) in enumerate(PRODUCTS):
                rows = slice(D * r, D * r + D)
                sp.dma_start(q_st[rows, slots(g), :], qkT[half, qp, :]).then_inc(stack_in[g % SETS], 16)
                sp.dma_start(k_st[rows, slots(g), :], qkT[half, 3 + kp, :]).then_inc(stack_in[g % SETS], 16)

        def max_rows(n, g):
            sp.wait_ge(max_ready, n * G + g + 1)
            for r in range(3):
                sp.dma_start(q_st[96 + r:97 + r, slots(g), :], max_part[:, g % 2, r, :]).then_inc(m_in[g % 2], 16)

        def send_rows(n, t):
            sp.wait_ge(r_ready, n * T + t + 1)
            sp.dma_start(middle[n, t * P:t * P + P, :], y[:, t, :]).then_inc(rows_out, 16)

        def load_residual(n, t):
            if t >= 2:
                sp.wait_ge(r_ready, n * T + t - 1)
            sp.dma_start(x_res[:, t % 2, :], x[(n + B - 1) % B, t * P:t * P + P, :]).then_inc(res_in[t % 2], 16)

        sp.wait_ge(const_a, STACKS_CLEAR)
        fill(0, 0)
        fill(0, 1)
        sp.wait_ge(side_full, side_at[("x", T - 1)] + 1)
        load_x(1)
        max_rows(0, 0)
        fill(0, 2)
        with sp.Fori(0, B) as b:
            for n in range(STEPS):
                if n % T == 1:
                    rows = ((n // T + 1) // G, (n // T + 1) % G)
                    g = fill_steps[n]
                    if g % 2 == 0:
                        max_rows(b + rows[0], rows[1])
                    sp.wait_ge(st_full, (b * STEPS + max(n - 1, 1)) * 2)
                    fill(b + (1 if n >= 21 else 0), g)
                    if g % 2:
                        max_rows(b + rows[0], rows[1])
                if n == 6:
                    load_residual(b, 0)
                    load_residual(b, 1)
                if n == 15:
                    load_residual(b, 2)
                    load_residual(b, 3)
                    send_rows(b, 0)
                    send_rows(b, 1)
                if n == 19:
                    send_rows(b, 2)
                    send_rows(b, 3)
                    sp.wait_ge(side_full, (b + 1) * SIDE + side_at[("x", T - 1)] + 1)
                    load_x(b + 2)
        load_residual(B, 0)
        load_residual(B, 1)
        sp.wait_ge(side_free, B * SIDE + len(ahead))
        sp.wait_ge(qk_l, (B * O + 2) * 2)
        sp.wait_ge(pv_done, PV0 + B * STEPS)
        sp.wait_ge(rot_free, B * ROT + sum(len(unit(h)) for h in range(LEAD)))
        sp.wait_ge(x_in, (B + 2) * 16)
        for g in range(SETS - 1):
            sp.wait_ge(stack_in[g], filled(B, g))
        sp.wait_ge(m_in[0], (B * (G // 2) + 1) * 48)
        for i in range(BESIDE):
            rounding.load(sp, i)

        def last_rows():
            for t in range(T):
                if t < T - 2:
                    load_residual(B, t + 2)
                send_rows(B, t)
            sp.wait_ge(rows_out, OUT0 + (B + 1) * T * 16)

        shared.last_rows = last_rows

    @block.gpsimd
    def _(pool):
        pool.memset(ident[:], 0.0).then_inc(const_a, 1)
        pool.wait_ge(const_a, 1)
        pool.affine_select(out=ident[:], in_=ident[:], compare_op=ALU.not_equal, fill=1.0, base=0,
                           pattern=[[-1, P]], channel_multiplier=1).then_inc(const_a, 1)
        pool.memset(minus_half[:], -0.5).then_inc(const_a, 1)
        pool.memset(q_st[:], 0.0).then_inc(const_a, 1)
        pool.memset(k_st[:], 0.0).then_inc(const_a, 1)
        pool.wait_ge(const_a, 5)
        pool.memset(k_st[96:99], -1.0).then_inc(const_a, 1)

        def inverse_std(name, n):
            a = norms[name]
            pool.wait_ge(ln_step[name], (n + 1) * AGGR)
            pool.tensor_tensor(a["rstd"][:], a["varpe"][:], minus_half[:], ALU.pow).then_inc(ln_rstd[name], 1)

        def project_low(n, what, o):
            i = (n * O + o) * 2 + "qk".index(what)
            part = 3 * "qk".index(what)
            pool.wait_ge(qk_m, i + 1)
            pool.tensor_tensor(qkT[:, part + 2, :], qk_rest[:], qkT[:, part + 1, :], ALU.subtract).then_inc(qk_l, 1)

        def normalise(k, o, last_use):
            if last_use is not None:
                pool.wait_ge(side_full, last_use)
            pool.wait_ge(den_rec, k + 1)
            pool.tensor_tensor(cT_h[:, o, :], ctx_raw[:], den[:], ALU.mult).then_inc(c_h, 1)
            pool.wait_ge(c_h, k + 1)
            pool.tensor_tensor(ctx_raw[:], ctx_raw[:], den[:], ALU.mult).then_inc(c_norm, 1)
            pool.wait_ge(c_norm, k + 1)
            pool.tensor_tensor(cT_l[:, o, :], ctx_raw[:], cT_h[:, o, :].bitcast(F32), ALU.subtract).then_inc(c_l, 1)

        def add_residual(n, t):
            pool.wait_ge(yn_ready, n * T + t + 1)
            pool.wait_ge(res_in[t % 2], (n * 2 + t // 2 + 1) * 16)
            pool.tensor_tensor(y[:, t, :], y[:, t, :], x_res[:, t % 2, :], ALU.add).then_inc(r_ready, 1)

        pool.wait_ge(const_a, STACKS_CLEAR)
        inverse_std("in", 0)
        pool.memset(v_one[:], 1.0).then_inc(const_a, 1)
        for item in start:
            if item[0] in "qk":
                project_low(0, *item)
            if item == ("k", 0):
                pool.memset(cT_h[:].bitcast(F32), 0.0).then_inc(const_a, 1)
                pool.memset(cT_l[:].bitcast(F32), 0.0).then_inc(const_a, 1)
                pool.memset(ctx_raw[:], 0.0).then_inc(const_a, 1)
                pool.memset(den[:], 1.0).then_inc(const_a, 1)
        pool.wait_ge(const_a, CONSTS)
        with pool.Fori(0, B) as b:
            for n in range(STEPS):
                if n == 1:
                    normalise(b * O, O - 1, None)
                if n % 8 == 1 and n > 1:
                    o = n // 8 - 1
                    normalise(b * O + 1 + o, o, b * SIDE + side_at[("o", T - 1)] + 1 if o == 0 else None)
                if n - 1 in side_steps and side_steps[n - 1][0] in "qk":
                    project_low(b + of_next(side_steps[n - 1], n - 1), *side_steps[n - 1])
                if n == 5:
                    inverse_std("in", b + 1)
                if n == 10:
                    inverse_std("out", b)
                if n in (13, 14):
                    for t in (0, 1) if n == 13 else (2,):
                        add_residual(b, t)
                if n == 16:
                    add_residual(b, 3)
        normalise(B * O, O - 1, None)
        for i in range(BESIDE - 1):
            rounding.take_magic(pool, i)
        inverse_std("out", B)
        rounding.take_magic(pool, BESIDE - 1)
        for t in range(T):
            add_residual(B, t)

    @block.scalar
    def _(act):
        act.sem_inc(p_full, PROBS0)
        act.preload_act_table_set("natural_log_exp_and_others")

        def weight_high(n):
            i = "qkvo".index(n)
            if n == "q":
                act.wait_ge(q_scaled, 1)
            else:
                act.wait_ge(w_in[n], 128 if n == "o" else 16)
            for c in range(KC):
                src, dst = probs[:, i % 2, c, :], w_h[n][:, c, :]
                if n in "qk":
                    src = src.rearrange("p (a h d) -> p a d h", h=GH, d=D)
                    dst = dst.rearrange("p (a d h) -> p a d h", h=GH, d=D)
                act.copy(dst, src).then_inc(w_high, 1)

        for n in "qkv":
            weight_high(n)
        act.wait_ge(b_in, 16 * (4 * GH + 2))
        act.mul(b_qk[:, 0, :], b_qk[:, 0, :], float(D) ** -0.5).then_inc(b_scaled, 1)
        act.wait_ge(b_scaled, 1)

        def side_high(n, item, at):
            what, i = item
            if what not in "xqk":
                return
            act.wait_ge(side_full, at + 1)
            if what == "x":
                act.copy(xT_h[:, :, i * P:i * P + P], side[:].rearrange("p (c t) -> p c t", c=KC)).then_inc(xTh, 1)
                return
            for g in (2 * i - 2, 2 * i - 1):
                if g >= 0:
                    act.wait_ge(stack_in[g % SETS], filled(n, g))
                elif not isinstance(n, int):
                    act.wait_ge(stack_in[g % SETS], filled(n - 1, g + G))
            part = 3 * "qk".index(what)
            act.activation(qkT[:, part, :], side[:], ACT.Identity, bias=b_qk[:, part // 3, i:i + 1]).then_inc(qk_h, 1)

        def side_middle(item, at):
            what, i = item
            if what in "qk":
                part = 3 * "qk".index(what)
                act.wait_ge(side_free, at + 1)
                act.copy(qkT[:, part + 1, :], qk_rest[:]).then_inc(qk_m, 1)

        def contexts_even(b, o):
            act.wait_ge(pv_done, PV0 + b * STEPS + (2 * o + 1) * T)
            act.wait_ge(c_l, b * O + o + 1)
            act.mul(ctx_raw[:], cps[:], half_mask[:, 0:1]).then_inc(c0_out, 1)
            act.mul(den[:], cps[:], half_mask[:, 1:2]).then_inc(c0_out, 1)

        def invert(k):
            act.wait_ge(den_sh, SHUF0 + k)
            act.activation(den[:], den[:], ACT.Ln).then_inc(den_ln, 1)
            act.wait_ge(den_ln, k + 1)
            act.activation(den[:], den[:], ACT.Exp, scale=-1.0).then_inc(den_rec, 1)

        for item in start:
            if item == ("w", "o"):
                weight_high("o")
            elif item in start_at:
                side_high(0, item, start_at[item])
                side_middle(item, start_at[item])
        act.wait_ge(const_v, 1)
        act.wait_ge(const_a, CONSTS)
        with act.Fori(0, B) as b:
            for n in range(STEPS):
                g, c = divmod(n, T)
                before = side_steps.get(n - 1)
                if before:
                    k = b + of_next(before, n - 1)
                    side_high(k, before, k * SIDE + side_at[before])
                if n == 1:
                    invert(b * O)
                if n % 8 == 1 and n > 1:
                    invert(b * O + n // 8)
                for u in range(2):
                    act.wait_ge(st_full, (b * STEPS + n) * 2 + u + 1)
                    act.wait_ge(pv_done, PV0 + b * STEPS + n - 1)
                    act.activation(probs[:, n % 2, 2 * u:2 * u + 2, :], work[:, 2 * u:2 * u + 2, :], ACT.Exp).then_inc(p_full, 1)
                if before:
                    side_middle(before, k * SIDE + side_at[before])
                if n % 8 == 4:
                    contexts_even(b, n // 8)
        invert(B * O)
        for i in range(BESIDE):
            rounding.overflow(act, i)

    @block.vector
    def _(dve):
        dve.wait_ge(const_a, 2)
        dve.tensor_reduce(half_mask[:], ident[:].rearrange("p (j e d) -> p e j d", j=GH, e=2), AX.XY, ALU.add).then_inc(const_v, 1)
        dve.sem_inc(c1_out, ODD0)
        dve.sem_inc(den_sh, SHUF0)
        dve.wait_ge(w_in["q"], 16)
        dve.tensor_scalar(probs[:, 0], probs[:, 0], float(D) ** -0.5, None, ALU.mult).then_inc(q_scaled, 1)
        dve.wait_ge(q_scaled, 1)

        def weight_low(n):
            i = "qkvo".index(n)
            for c in range(KC):
                dve.wait_ge(w_high, i * KC + c + 1)
                src, high, dst = probs[:, i % 2, c, :], w_h[n][:, c, :].bitcast(F32), w_l[n][:, c, :]
                if n in "qk":
                    src = src.rearrange("p (a h d) -> p a d h", h=GH, d=D)
                    high, dst = (a.rearrange("p (a d h) -> p a d h", h=GH, d=D) for a in (high, dst))
                last = dve.tensor_tensor(dst, src, high, ALU.subtract)
            last.then_inc(w_split, 1)

        def stats(name, rows, t):
            dve.bn_stats(norms[name]["stats"][:, t, :], rows[:, t, :]).then_inc(ln_stat[name], 1)

        def moments(name, n):
            a = norms[name]
            aggregate(dve, n, T, H, a["stats"], a["mean"], a["spread"], a["varpe"], ln_stat[name], ln_step[name])

        def normalise(name, rows, done, n):
            dve.wait_ge(ln_rstd[name], n + 1)
            for t in range(T):
                dve.tensor_scalar(rows[:, t, :], rows[:, t, :], norms[name]["mean"][:, t:t + 1],
                                  norms[name]["rstd"][:, t:t + 1], ALU.subtract, ALU.mult).then_inc(done, 1)

        def take(n, item, b=None):
            what, i = item
            at = start_at[item] if b is None else n * SIDE + side_at[item]
            if what == "x":
                dve.wait_ge(xTh, n * T + i + 1)
                toks = slice(i * P, i * P + P)
                dve.tensor_tensor(xT_l[:, :, toks], side[:].rearrange("p (c t) -> p c t", c=KC),
                                  xT_h[:, :, toks].bitcast(F32), ALU.subtract).then_inc(side_free, 1)
            elif what == "v":
                dve.wait_ge(side_full, at + 1)
                if b is not None:
                    dve.wait_ge(pv_done, PV0 + n * STEPS + i - T + 1)
                for e in range(2):
                    dst = v_one[:, i].rearrange("p (a e j) w -> p e a j w", e=2, j=GH)[:, e, :, :, e * D:e * D + D]
                    src, bias = (a.rearrange("p (a e j d) -> p e a j d", e=2, j=GH, d=D)[:, e] for a in (side[:], bv_rows[:]))
                    dve.tensor_tensor(dst, src, bias, ALU.add).then_inc((v_half, side_free)[e], 1)
            elif what == "o":
                take_out(at, n, i)
            else:
                k = (n * O + i) * 2 + "qk".index(what)
                part = 3 * "qk".index(what)
                dve.wait_ge(qk_h, k + 1)
                if not (isinstance(k, int) and k == 0):
                    dve.wait_ge(qk_l, k)
                dve.scalar_tensor_tensor(qk_rest[:], side[:], b_qk[:, part // 3, i:i + 1], qkT[:, part, :],
                                         ALU.add, ALU.subtract).then_inc(side_free, 1)

        def take_out(at, n, t):
            dve.wait_ge(side_full, at + 1)
            dve.wait_ge(rows_out, OUT0 + n * T * 16)
            dve.tensor_tensor(y[:, t, :], side[:], bo_rows[:], ALU.add).then_inc(side_free, 1)

        def reduce_maxima(n, item):
            at = n * ROT + rot_at[item]
            bank = rot[rot_at[item] % 2]
            dve.wait_ge(rot_full, at + 1)
            if item[0] == "s":
                _, g, j, qc = item
                dve.tensor_reduce(maxima[:, g % 2, j * T + qc:j * T + qc + 1], bank[:], AX.X, ALU.max).then_inc(rot_free, 1)
                return
            g = item[1]
            k = n * G + g
            rows = bank[0:GH * T, 0:P]
            if g >= 2:
                dve.wait_ge(m_in[g % 2], (n * (G // 2) + g // 2) * 48)
            elif not isinstance(n, int):
                dve.wait_ge(m_in[g % 2], (n * (G // 2)) * 48) if g == 0 else dve.wait_ge(m_in[0], (n * (G // 2) + 1) * 48)
            dve.tensor_copy(max_part[:, g % 2, 0, :], rows).then_inc(max_step, 1)
            dve.wait_ge(max_step, k * 2 + 1)
            dve.tensor_tensor(max_rest[:], rows, max_part[:, g % 2, 0, :], ALU.subtract).then_inc(rot_free, 1)
            dve.wait_ge(rot_free, at + 1)
            dve.tensor_copy(max_part[:, g % 2, 1, :], max_rest[:]).then_inc(max_step, 1)
            dve.wait_ge(max_step, k * 2 + 2)
            dve.tensor_tensor(max_part[:, g % 2, 2, :], max_rest[:], max_part[:, g % 2, 1, :], ALU.subtract).then_inc(max_ready, 1)

        def contexts_odd(b, o):
            k = b * O + o
            dve.wait_ge(pv_done, PV0 + b * STEPS + (2 * o + 2) * T)
            dve.wait_ge(c0_out, (k + 1) * 2)
            dve.scalar_tensor_tensor(den[:], cps[:], half_mask[:, 0:1], den[:], ALU.mult, ALU.add).then_inc(c1_out, 1)
            dve.wait_ge(c1_out, ODD0 + k * 2 + 1)
            dve.scalar_tensor_tensor(ctx_raw[:], cps[:], half_mask[:, 1:2], ctx_raw[:], ALU.mult, ALU.add).then_inc(c1_out, 1)
            dve.stream_shuffle(den[:], den[:], [(i + D) % 32 for i in range(32)]).then_inc(den_sh, 1)

        weight_low("q")
        weight_low("k")
        dve.wait_ge(x_in, 16)
        for t in range(T):
            stats("in", x_rows, t)
        moments("in", 0)
        weight_low("v")
        normalise("in", x_rows, xn_ready, 0)
        for item in start:
            if item[0] == "r":
                for i in unit(item[1]):
                    reduce_maxima(0, i)
            elif item == ("w", "o"):
                weight_low("o")
            else:
                if item == ("q", 0):
                    dve.wait_ge(b_scaled, 1)
                if item == ("v", 0):
                    dve.wait_ge(const_a, ONES)
                take(0, item)
        dve.wait_ge(const_a, CONSTS)
        with dve.Fori(0, B) as b:
            for n in range(STEPS):
                first, *others = rot_step(n)
                reduce_maxima(b + first[1], first[0])
                if n - 1 in side_steps:
                    item = side_steps[n - 1]
                    take(b + of_next(item, n - 1), item, b)
                    if item[0] == "o":
                        dve.wait_ge(side_free, b * SIDE + side_at[item] + 1)
                        stats("out", y, item[1])
                for item, later in others:
                    reduce_maxima(b + later, item)
                if n == 1:
                    dve.wait_ge(x_in, (b + 2) * 16)
                if n in (1, 2):
                    stats("in", x_rows, 2 * (n - 1))
                    stats("in", x_rows, 2 * (n - 1) + 1)
                if n == 3:
                    moments("in", b + 1)
                if n == 7:
                    normalise("in", x_rows, xn_ready, b + 1)
                if n == 9:
                    moments("out", b)
                if n == 11:
                    normalise("out", y, yn_ready, b)
                if n % 8 == 0 and n:
                    contexts_odd(b, n // 8 - 1)
            take(b + 1, ("v", 2), b)
            contexts_odd(b, O - 1)
        for i in range(BEFORE):
            rounding.quantise(dve, i)
        for t in range(T):
            take_out(B * SIDE + len(ahead) + t, B, t)
            dve.wait_ge(side_free, B * SIDE + len(ahead) + t + 1)
            stats("out", y, t)
            rounding.quantise(dve, BEFORE + t)
        moments("out", B)
        rounding.quantise(dve, BESIDE - 1)
        normalise("out", y, yn_ready, B)

    @block.tensor
    def _(pe):
        pe.sem_inc(pv_done, PV0)
        pe.sem_inc(rows_out, OUT0)
        pe.wait_ge(const_a, IDENT)

        def product(out, left, right, first, last):
            for i, (a, c) in enumerate(((0, 0), (1, 0), (0, 1))):
                mm = pe.matmul(out, left[a], right[c], start=first and i == 0, stop=last and i == 2)
            return mm

        def side_piece(at, n, item, c):
            what, i = item
            if c == 0 and not (isinstance(at, int) and at == 0):
                pe.wait_ge(side_free, at)
            toks = slice(i * P, i * P + P)
            if what == "x":
                if c == 0:
                    pe.wait_ge(xn_ready, n * T + i + 1)
                mm = pe.transpose(side[:, c * P:c * P + P], x_rows[:, i, c * P:c * P + P], ident[:])
            elif what in "qk":
                mm = product(side[:], (w_h[what][:, c, toks], w_l[what][:, c, toks]),
                             (xT_h[:, c, :], xT_l[:, c, :]), c == 0, c == KC - 1)
            elif what == "v":
                mm = product(side[:], (xT_h[:, c, toks], xT_l[:, c, toks]),
                             (w_h["v"][:, c, :], w_l["v"][:, c, :]), c == 0, c == KC - 1)
            else:
                if c == 0:
                    pe.wait_ge(c_l, n * O + 1)
                mm = product(side[:], (cT_h[:, c, toks], cT_l[:, c, toks]),
                             (w_h["o"][:, c, :], w_l["o"][:, c, :]), c == 0, c == KC - 1)
            if c == KC - 1:
                mm.then_inc(side_full, 1)

        def rot_item(n, item):
            at = n * ROT + rot_at[item]
            bank = rot[rot_at[item] % 2]
            if not (isinstance(at, int) and at < 2):
                pe.wait_ge(rot_free, at - 1)
            if item[0] == "s":
                _, g, j, qc = item
                if j == 0 and qc == 0:
                    pe.wait_ge(stack_in[g % SETS], filled(n, g))
                s = (g % SETS) * GH + j
                mm = pe.matmul(bank[:], q_st[:, s, qc * P:qc * P + P], k_st[:, s, :], start=True, stop=True)
            else:
                pe.wait_ge(rot_free, at)
                mm = pe.transpose(bank[0:GH * T, 0:P], maxima[:, item[1] % 2, :], ident[:])
            mm.then_inc(rot_full, 1)

        def scores(b, n, u):
            g, c = divmod(n, T)
            pe.wait_ge(p_full, PROBS0 + (b * STEPS + n) * 2 + u - 1)
            if c == 0 and u == 0:
                pe.wait_ge(m_in[g % 2], (b * (G // 2) + g // 2 + 1) * 48)
            for j in range(2 * u, 2 * u + 2):
                s = (g % SETS) * GH + j
                mm = pe.matmul(work[:, j, :], k_st[:, s, c * P:c * P + P], q_st[:, s, :], start=True, stop=True)
            mm.then_inc(st_full, 1)

        def contexts(b, n):
            g, c = divmod(n, T)
            pe.wait_ge(p_full, PROBS0 + (b * STEPS + n + 1) * 2)
            if g == 0:
                pe.wait_ge(side_free, b * SIDE + side_at[("v", c)] + 1)
            if c == 0:
                pe.wait_ge(*((c0_out, (b * O + g // 2 + 1) * 2) if g % 2 else (c1_out, ODD0 + (b * O + g // 2) * 2)))
            for j in range(GH):
                mm = pe.matmul(cps[32 * j:32 * j + 32, :], v_one[:, c, GH * g + j, :],
                               probs[:, n % 2, j, :], start=(c == 0), stop=(c == T - 1))
            mm.then_inc(pv_done, 1)

        for item in start:
            if item[0] == "r":
                for i in unit(item[1]):
                    rot_item(0, i)
            elif item in start_at:
                if item[0] in "qkv":
                    pe.wait_ge(w_split, "qkv".index(item[0]) + 1)
                for c in range(KC):
                    side_piece(start_at[item], 0, item, c)
        pe.wait_ge(w_split, 4)
        pe.wait_ge(const_a, CONSTS)
        with pe.Fori(0, B) as b:
            for n in range(STEPS):
                items = rot_step(n)
                cut = [len(items) * k // 5 for k in range(5 + 1)]
                side_item = side_steps.get(n)
                later = b + of_next(side_item, n) if side_item else 0

                def quarter(k):
                    for item, nxt in items[cut[k]:cut[k + 1]]:
                        rot_item(b + nxt, item)

                def piece(c):
                    if side_item:
                        side_piece(later * SIDE + side_at[side_item], later, side_item, c)

                quarter(0)
                scores(b, n, 0)
                quarter(1)
                scores(b, n, 1)
                quarter(2)
                if n:
                    contexts(b, n - 1)
                piece(0)
                quarter(3)
                piece(1)
                quarter(4)
                piece(2)
                piece(3)
            contexts(b, STEPS - 1)
        for t in range(T):
            for c in range(KC):
                side_piece(B * SIDE + len(ahead) + t, B, ("o", t), c)

    return shared


def ffn_pass(nc, ctx, block, shared, ident, middle, gate_s, up_s, down_s, out):
    B, S, H = out.shape
    T = S // P
    KC = H // P
    rounding = shared.rounding
    gate_q, up_q, down_q = rounding.gate_q, rounding.up_q, rounding.down_q
    F = rounding.F
    XS = 1024.0
    QF = rounding.QF

    sb = lambda name, shape, dt=F32: ctx.enter_context(nc.sbuf_tensor(name, shape, dt))
    ps = lambda name, shape: ctx.enter_context(nc.psum_tensor(name, shape, F32))
    sem = lambda name: ctx.enter_context(nc.semaphore(name))

    gs_in = sb("gate_scale_in", [P, F])
    us_in = sb("up_scale_in", [P, F])
    gs = sb("gate_scale", [P, F])
    us = sb("up_scale", [P, F])
    ds_rows = sb("down_scale_rows", [P, H])

    x_rows = sb("x_rows_ffn", [P, T, H])
    x_res = sb("x_residual_ffn", [P, T, H])
    y = sb("y_ffn", [P, T, H])
    xT_h = sb("xT_high_ffn", [P, KC, S], F16)
    xT_l = sb("xT_low_ffn", [P, KC, S], F16)
    gate = sb("gate", [P, 2, S])
    fuse = sb("fuse", [P, 2, S])
    fuse_h = sb("fuse_high", [P, 2, S], F32R)
    fuse_l = sb("fuse_low", [P, 2, S], F32R)
    norms = {n: {k: sb(f"{k}_{n}_ffn", s) for k, s in (("stats", [P, T, 6]), ("mean", [P, T]), ("spread", [P, 3, T]),
                                                       ("varpe", [P, T]), ("rstd", [P, T]))} for n in ("in", "out")}

    ring = ps("ring", [P, 2, 2, S])
    acc = ps("down_sums", [P, T, H])

    s_in = sem("scales_in")
    s_ready = sem("scales_ready")
    x_in = sem("x_in_ffn")
    res_in = sem("x_residual_in_ffn")
    ln_stat = {n: sem(f"ln_{n}_stat_ffn") for n in ("in", "out")}
    ln_step = {n: sem(f"ln_{n}_step_ffn") for n in ("in", "out")}
    ln_rstd = {n: sem(f"ln_{n}_rstd_ffn") for n in ("in", "out")}
    xn_ready = sem("xn_ready_ffn")
    xT_full = sem("xT_in_ring")
    xTh = sem("xT_high_ready_ffn")
    xTl = sem("xT_low_ready_ffn")
    gu_full = sem("gate_up_in_ring")
    silu = sem("gate_ready")
    fused = sem("fuse_ready")
    fh = sem("fuse_high_ready")
    fl = sem("fuse_low_ready")
    down_done = sem("down_added")
    y_ready = sem("y_ready_ffn")
    yn_ready = sem("y_normalised_ffn")
    r_ready = sem("row_sum_ready_ffn")
    rows_out = sem("rows_out_ffn")

    START = rounding.gate_up_jobs[0] + 2

    def jobs_at(f):
        lo = START + f * 3
        return range(min(lo, rounding.count), min(lo + 3, rounding.count))

    assert jobs_at(F - 1).stop == rounding.count and jobs_at(QF - 1).stop >= rounding.gate_up_jobs[1] + 2

    @block.sync
    def _(sp):
        sp.wait_ge(shared.rows_out, shared.rows_before_last)
        sp.dma_start(x_rows[:], middle[1].rearrange("(t p) h -> p t h", p=P)).then_inc(x_in, 16)
        sp.dma_start(gs_in[:], gate_s.rearrange("(f p) -> p f", p=P), allow_slow_non_contiguous=True).then_inc(s_in, 16)
        sp.dma_start(us_in[:], up_s.rearrange("(f p) -> p f", p=P), allow_slow_non_contiguous=True).then_inc(s_in, 16)
        sp.dma_start(ds_rows[:], down_s.partition_broadcast(P)).then_inc(s_in, 16)

        def load_x(n):
            sp.wait_ge(xT_full, (n + 1) * KC)
            sp.dma_start(x_rows[:], middle[(n + 1) % B + 1].rearrange("(t p) h -> p t h", p=P)).then_inc(x_in, 16)

        def end_rows(n):
            sp.dma_start(x_res[:], middle[n + 1].rearrange("(t p) h -> p t h", p=P)).then_inc(res_in, 16)
            for t in range(T):
                sp.wait_ge(r_ready, n * T + t + 1)
                sp.dma_start(out[n, t * P:t * P + P, :], y[:, t, :]).then_inc(rows_out, 16)

        for i in range(shared.rounded, START):
            rounding.load(sp, i)
        shared.last_rows()
        load_x(0)
        for i in range(START, rounding.count):
            rounding.load(sp, i)
        with sp.Fori(1, B) as b:
            load_x(b)
            end_rows(b - 1)
        end_rows(B - 1)
        sp.wait_ge(rows_out, B * T * 16)
        sp.wait_ge(x_in, (B + 1) * 16)

    @block.gpsimd
    def _(pool):
        def inverse_std(name, n):
            pool.wait_ge(ln_step[name], (n + 1) * AGGR)
            pool.tensor_tensor(norms[name]["rstd"][:], norms[name]["varpe"][:], shared.minus_half[:], ALU.pow).then_inc(ln_rstd[name], 1)

        def batch(b, first):
            for f in range(F):
                if first:
                    for i in jobs_at(f):
                        rounding.take_magic(pool, i)
                elif f == 1:
                    inverse_std("out", b - 1)
                if f == 5:
                    inverse_std("in", b + 1)
                pool.wait_ge(fh, b * F + f + 1)
                pool.tensor_tensor(fuse_l[:, f % 2, :], fuse[:, f % 2, :], fuse_h[:, f % 2, :].bitcast(F32), ALU.subtract).then_inc(fl, 1)

        inverse_std("in", 0)
        for i in range(shared.rounded, START):
            rounding.take_magic(pool, i)
        batch(0, True)
        with pool.Fori(1, B) as b:
            batch(b, False)
        inverse_std("out", B - 1)

    @block.scalar
    def _(act):
        def x_high(n):
            for c in range(KC):
                act.wait_ge(xT_full, n * KC + c + 1)
                act.mul(xT_h[:, c, :], ring[:, c // 2, c % 2, :], XS).then_inc(xTh, 1)

        def batch(b, first):
            for f in range(F):
                k = b * F + f
                if first:
                    for i in jobs_at(f):
                        rounding.overflow(act, i)
                act.wait_ge(gu_full, k * 2 + 1)
                act.activation(gate[:, f % 2, :], ring[:, f % 2, 0, :], ACT.Silu, scale=gs[:, f:f + 1]).then_inc(silu, 1)
                act.wait_ge(fused, k + 1)
                if not first or f >= 2:
                    act.wait_ge(down_done, k - 1)
                act.copy(fuse_h[:, f % 2, :], fuse[:, f % 2, :]).then_inc(fh, 1)
            x_high(b + 1)

        act.preload_act_table(ACT.Silu)
        for i in range(shared.rounded, START):
            rounding.overflow(act, i)
        act.wait_ge(s_ready, 2)
        x_high(0)
        batch(0, True)
        with act.Fori(1, B) as b:
            batch(b, False)

    @block.vector
    def _(dve):
        def stats(name, rows):
            for t in range(T):
                if name == "out":
                    dve.wait_ge(*y_at[t])
                dve.bn_stats(norms[name]["stats"][:, t, :], rows[:, t, :]).then_inc(ln_stat[name], 1)

        def moments(name, n):
            a = norms[name]
            aggregate(dve, n, T, H, a["stats"], a["mean"], a["spread"], a["varpe"], ln_stat[name], ln_step[name])

        def normalise(name, rows, done, n):
            dve.wait_ge(ln_rstd[name], n + 1)
            for t in range(T):
                dve.tensor_scalar(rows[:, t, :], rows[:, t, :], norms[name]["mean"][:, t:t + 1],
                                  norms[name]["rstd"][:, t:t + 1], ALU.subtract, ALU.mult).then_inc(done, 1)

        def add_residual(n):
            dve.wait_ge(res_in, (n + 1) * 16)
            for t in range(T):
                dve.wait_ge(yn_ready, n * T + t + 1)
                dve.tensor_tensor(y[:, t, :], y[:, t, :], x_res[:, t, :], ALU.add).then_inc(r_ready, 1)

        def x_low(n):
            for c in range(KC):
                dve.wait_ge(xTh, n * KC + c + 1)
                dve.scalar_tensor_tensor(xT_l[:, c, :], ring[:, c // 2, c % 2, :], XS, xT_h[:, c, :],
                                         ALU.mult, ALU.subtract).then_inc(xTl, 1)

        y_at = [None] * T

        def batch(b, first):
            for f in range(F):
                k = b * F + f
                if first:
                    for i in jobs_at(f):
                        rounding.quantise(dve, i)
                elif f == 0:
                    moments("out", b - 1)
                elif f == 2:
                    normalise("out", y, yn_ready, b - 1)
                    add_residual(b - 1)
                if f == 3:
                    dve.wait_ge(x_in, (b + 2) * 16)
                    stats("in", x_rows)
                if f == 4:
                    moments("in", b + 1)
                if f == 7:
                    normalise("in", x_rows, xn_ready, b + 1)
                dve.wait_ge(gu_full, k * 2 + 2)
                dve.wait_ge(silu, k + 1)
                if not first or f >= 2:
                    dve.wait_ge(fl, k - 1)
                dve.scalar_tensor_tensor(fuse[:, f % 2, :], ring[:, f % 2, 1, :], us[:, f:f + 1], gate[:, f % 2, :],
                                         ALU.mult, ALU.mult).then_inc(fused, 1)
            x_low(b + 1)
            dve.wait_ge(down_done, (b + 1) * F)
            if not first:
                dve.wait_ge(rows_out, b * T * 16)
            for t in range(T):
                dve.tensor_tensor(y[:, t, :], acc[:, t, :], ds_rows[:], ALU.mult).then_inc(y_ready, 1)
                y_at[t] = (y_ready, b * T + t + 1)
            stats("out", y)

        dve.wait_ge(s_in, 48)
        dve.tensor_scalar(gs[:], gs_in[:], 1.0 / XS, None, ALU.mult).then_inc(s_ready, 1)
        dve.tensor_scalar(us[:], us_in[:], 1.0 / XS, None, ALU.mult).then_inc(s_ready, 1)
        dve.wait_ge(x_in, 16)
        stats("in", x_rows)
        moments("in", 0)
        for i in range(shared.rounded, START):
            rounding.quantise(dve, i)
        normalise("in", x_rows, xn_ready, 0)
        x_low(0)
        batch(0, True)
        with dve.Fori(1, B) as b:
            batch(b, False)
        moments("out", B - 1)
        normalise("out", y, yn_ready, B - 1)
        add_residual(B - 1)

    @block.tensor
    def _(pe):
        def transposes(n, half, first):
            if half == 0:
                pe.wait_ge(xn_ready, (n + 1) * T)
            if not first:
                pe.wait_ge(fused, n * F - 1 + half)
            for c in (2 * half, 2 * half + 1):
                for t in range(T):
                    mm = pe.transpose(ring[:, half, c % 2, t * P:t * P + P], x_rows[:, t, c * P:c * P + P], ident[:])
                mm.then_inc(xT_full, 1)

        def gate_up(b, f, first):
            k = b * F + f
            if first and f % QF == 0:
                pe.wait_ge(rounding.quant, rounding.gate_up_jobs[f // QF])
            if f == 0:
                pe.wait_ge(xTl, (b + 1) * KC)
            elif f >= 2:
                pe.wait_ge(fused, k - 1)
            for w, weight in enumerate((gate_q, up_q)):
                for c in range(KC):
                    for i, part in enumerate((xT_h, xT_l)):
                        mm = pe.matmul(ring[:, f % 2, w, :], weight[:, c, f * P:f * P + P], part[:, c, :],
                                       start=(c == 0 and i == 0), stop=(c == KC - 1 and i == 1))
                mm.then_inc(gu_full, 1)

        def down(b, f, first):
            if first:
                pe.wait_ge(rounding.quant, rounding.down_job[f])
                if f == 0:
                    pe.wait_ge(shared.side_free, shared.side_items)
            elif f == 0:
                pe.wait_ge(y_ready, b * T)
            pe.wait_ge(fl, b * F + f + 1)
            for t in range(T):
                toks = slice(t * P, t * P + P)
                for i, part in enumerate((fuse_h, fuse_l)):
                    mm = pe.matmul(acc[:, t, :], part[:, f % 2, toks], down_q[:, f, :],
                                   start=(f == 0 and i == 0), stop=(f == F - 1 and i == 1))
            mm.then_inc(down_done, 1)

        def batch(b, first):
            for f in range(F):
                gate_up(b, f, first)
                if 0 < f < F - 1:
                    down(b, f - 1, first)
            transposes(b + 1, 0, False)
            down(b, F - 2, first)
            transposes(b + 1, 1, False)
            down(b, F - 1, first)

        transposes(0, 0, True)
        transposes(0, 1, True)
        batch(0, True)
        with pe.Fori(1, B) as b:
            batch(b, False)


_INS = ['L0_attn_hidden_states', 'L0_attn_Wq', 'L0_attn_bq', 'L0_attn_Wk', 'L0_attn_bk', 'L0_attn_Wv', 'L0_attn_bv',
        'L0_attn_Wo', 'L0_attn_bo', 'L0_ffn_gate_w', 'L0_ffn_up_w', 'L0_ffn_down_w', 'L0_ffn_gate_scale',
        'L0_ffn_up_scale', 'L0_ffn_down_scale']


def kernel(**inputs):
    import numpy as np
    import concourse.bacc as bacc
    from concourse.bass_utils import run_bass_kernel_spmd

    nc = bacc.Bacc("TRN2", target_bir_lowering=False, num_devices=1)
    arrays, args = {}, []
    for name in _INS:
        a = np.ascontiguousarray(inputs[name])
        arrays[f"in_{name}"] = a
        args.append(nc.dram_tensor(f"in_{name}", a.shape, mybir.dt.from_np(a.dtype), kind="ExternalInput").ap())
    shape = inputs[_INS[0]].shape
    out = nc.dram_tensor("out_rows", shape, F32, kind="ExternalOutput").ap()
    layer(nc, *args, out)
    r = run_bass_kernel_spmd(nc, [arrays], core_ids=[0])
    return r.results[0]["out_rows"]
```

```python
from contextlib import ExitStack

import concourse.bass as bass
from concourse import mybir

F32 = mybir.dt.float32
F32R = mybir.dt.float32r
F16 = mybir.dt.float16
BF16 = mybir.dt.bfloat16
I32 = mybir.dt.int32
ALU = mybir.AluOpType
ACT = mybir.ActivationFunctionType
AX = mybir.AxisListType

P = 128
NH = 32
D = 16
GH = 4
EPS = 1e-5
SETS = 4
LEAD = 7
IDENT, STACKS_CLEAR, ONES, CONSTS = 2, 7, 8, 12
PRODUCTS = ((0, 0), (0, 1), (0, 2), (1, 0), (1, 1), (2, 0))
FILL = (1 + 2 * len(PRODUCTS)) * 16
AGGR = 7


def aggregate(dve, n, T, width, stats, mean, spread, varpe, stat_done, step_done):
    dve.wait_ge(stat_done, n * T + T)
    dve.tensor_tensor(spread[:, 0, :], stats[:, :, 1], stats[:, :, 4], ALU.add).then_inc(step_done, 1)
    dve.tensor_tensor(spread[:, 1, :], stats[:, :, 1], stats[:, :, 4], ALU.subtract).then_inc(step_done, 1)
    dve.tensor_tensor(spread[:, 2, :], stats[:, :, 2], stats[:, :, 5], ALU.add).then_inc(step_done, 1)
    dve.wait_ge(step_done, n * AGGR + 2)
    dve.tensor_scalar(mean[:], spread[:, 0, :], 0.5, None, ALU.mult).then_inc(step_done, 1)
    dve.tensor_tensor(varpe[:], spread[:, 1, :], spread[:, 1, :], ALU.mult).then_inc(step_done, 1)
    dve.wait_ge(step_done, n * AGGR + 5)
    dve.scalar_tensor_tensor(varpe[:], varpe[:], width / 4.0, spread[:, 2, :], ALU.mult, ALU.add).then_inc(step_done, 1)
    dve.wait_ge(step_done, n * AGGR + 6)
    dve.tensor_scalar(varpe[:], varpe[:], 1.0 / width, EPS, ALU.mult, ALU.add).then_inc(step_done, 1)


def layer(nc, x, Wq, bq, Wk, bk, Wv, bv, Wo, bo, gate_w, up_w, down_w, gate_s, up_s, down_s, out):
    with ExitStack() as ctx:
        B, S, H = x.shape
        middle = nc.dram_tensor("middle_rows", [B + 1, S, H], F32, kind="Internal").ap()
        ident = ctx.enter_context(nc.sbuf_tensor("ident", [P, P], F32))
        with nc.Block() as block:
            shared = attention_pass(nc, ctx, block, ident, x, Wq, bq, Wk, bk, Wv, bv, Wo, bo,
                                    (gate_w, up_w, down_w), middle)
            ffn_pass(nc, ctx, block, shared, ident, middle, gate_s, up_s, down_s, out)


class Shared:
    pass


def weight_rounding(nc, ctx, gate_w, up_w, down_w):
    H, I = gate_w.shape
    KC = H // P
    F = I // P
    QF = H // P
    RAW = 8

    sb = lambda name, shape, dt=F32: ctx.enter_context(nc.sbuf_tensor(name, shape, dt))
    sem = lambda name: ctx.enter_context(nc.semaphore(name))

    gate_q = sb("gate_q", [P, KC, I], F16)
    up_q = sb("up_q", [P, KC, I], F16)
    down_q = sb("down_q", [P, F, H], F32R)
    w_raw = sb("w_raw", [P, RAW, H])
    w_magic = sb("w_magic", [P, 2, H])
    w_sum = sb("w_sum", [P, 2, H])
    w_round = sb("w_rounded", [P, 2, H])
    w_big = sb("w_overflow", [P, 2, H])

    raw_in = [sem(f"w_raw_in{i}") for i in range(RAW)]
    power = sem("w_power_ready")
    magic = sem("w_magic_ready")
    summed = sem("w_summed")
    rounded = sem("w_rounded_ready")
    big = sem("w_overflow_ready")
    quant = sem("w_quantised")

    jobs, gate_up_jobs, down_job = [], {}, {}
    for q in range(F // QF):
        cols = slice(q * H, q * H + H)
        for c in range(KC):
            jobs.append((gate_w[c * P:c * P + P, cols], gate_q[:, c, cols]))
            jobs.append((up_w[c * P:c * P + P, cols], up_q[:, c, cols]))
        gate_up_jobs[q] = len(jobs)
        for f in range(q * QF, q * QF + QF):
            jobs.append((down_w[f * P:f * P + P, :], down_q[:, f, :]))
            down_job[f] = len(jobs)

    def load(sp, i):
        if i >= RAW:
            sp.wait_ge(summed, i - RAW + 1)
        sp.dma_start(w_raw[:, i % RAW, :], jobs[i][0]).then_inc(raw_in[i % RAW], 16)

    def add_magic(dve, i):
        dve.wait_ge(raw_in[i % RAW], (i // RAW + 1) * 16)
        if i >= 2:
            dve.wait_ge(rounded, i - 1)
        w, m = w_raw[:, i % RAW, :], w_magic[:, i % 2, :]
        dve.tensor_scalar(m.bitcast(I32), w.bitcast(I32), 0x7F800000, None, ALU.bitwise_and).then_inc(power, 1)
        dve.wait_ge(power, i + 1)
        dve.tensor_scalar(m, m, 2.0 ** -6, 1.5 * 2.0 ** 20, ALU.max, ALU.mult).then_inc(magic, 1)
        dve.wait_ge(magic, i + 1)
        dve.tensor_tensor(w_sum[:, i % 2, :], w, m, ALU.add).then_inc(summed, 1)

    def take_magic(pool, i):
        pool.wait_ge(summed, i + 1)
        if i >= 2:
            pool.wait_ge(quant, i - 1)
        pool.tensor_tensor(w_round[:, i % 2, :], w_sum[:, i % 2, :], w_magic[:, i % 2, :], ALU.subtract).then_inc(rounded, 1)

    def overflow(act, i):
        act.wait_ge(rounded, i + 1)
        if i >= 2:
            act.wait_ge(quant, i - 1)
        act.mul(w_big[:, i % 2, :], w_round[:, i % 2, :], 1.1 * 2.0 ** 119).then_inc(big, 1)

    def store(dve, i):
        dve.wait_ge(big, i + 1)
        dve.scalar_tensor_tensor(jobs[i][1], w_big[:, i % 2, :], 0.0, w_round[:, i % 2, :], ALU.mult, ALU.add).then_inc(quant, 1)

    def quantise(dve, i):
        add_magic(dve, i)
        if i >= 1:
            store(dve, i - 1)
        if i == len(jobs) - 1:
            store(dve, i)

    r = Shared()
    r.F, r.QF, r.RAW, r.count, r.gate_up_jobs, r.down_job = F, QF, RAW, len(jobs), gate_up_jobs, down_job
    r.quant, r.gate_q, r.up_q, r.down_q = quant, gate_q, up_q, down_q
    r.load, r.quantise, r.take_magic, r.overflow = load, quantise, take_magic, overflow
    return r


def attention_pass(nc, ctx, block, ident, x, Wq, bq, Wk, bk, Wv, bv, Wo, bo, ffn_weights, middle):
    B, S, H = x.shape
    T = S // P
    KC = H // P
    G = NH // GH
    O = G // 2
    STEPS = G * T

    turns = ExitStack()
    sb = lambda name, shape, dt=F32: turns.enter_context(nc.sbuf_tensor(name, shape, dt))
    keep = lambda name, shape, dt=F32: ctx.enter_context(nc.sbuf_tensor(name, shape, dt, side="right"))
    ps = lambda name, shape: turns.enter_context(nc.psum_tensor(name, shape, F32))
    sem = lambda name: ctx.enter_context(nc.semaphore(name))

    w_h = {n: (keep if n == "o" else sb)(f"w{n}_high", [P, KC, H], F32R) for n in "qkvo"}
    w_l = {n: (keep if n == "o" else sb)(f"w{n}_low", [P, KC, H], F32R) for n in "qkvo"}
    b_qk = keep("bias_qk", [P, 2, O])
    bv_rows = sb("bias_v_rows", [P, H])
    bo_rows = keep("bias_o_rows", [P, H])
    half_mask = keep("half_mask", [P, 2])
    minus_half = keep("minus_half", [P, T])

    x_rows = sb("x_rows", [P, T, H])
    x_res = keep("x_residual", [P, 2, H])
    y = keep("y", [P, T, H])
    xT_h = sb("xT_high", [P, KC, S], F32R)
    xT_l = sb("xT_low", [P, KC, S], F32R)
    qkT = sb("qkT", [P, 6, S], BF16)
    qk_rest = sb("qk_rest", [P, S])
    v_one = sb("v_one", [P, T, NH, 2 * D])
    q_st = sb("q_stack", [P, SETS * GH, S], BF16)
    k_st = sb("k_stack", [P, SETS * GH, S], BF16)
    probs = sb("probs", [P, 2, GH, S])
    cT_h = keep("ctxT_high", [P, O, S], F32R)
    cT_l = keep("ctxT_low", [P, O, S], F32R)
    ctx_raw = keep("ctx_raw", [P, 2, S])
    den = keep("denominators", [P, 2, S])
    rec = keep("reciprocals", [P, S])
    two = keep("two", [P, 1])
    maxima = sb("maxima", [P, 2, GH * T])
    max_part = sb("max_parts", [GH * T, 2, 3, P], BF16)
    max_rest = sb("max_rest", [GH * T, P])
    norms = {n: {k: keep(f"{k}_{n}", s) for k, s in (("stats", [P, T, 6]), ("mean", [P, T]), ("spread", [P, 3, T]),
                                                   ("varpe", [P, T]), ("rstd", [P, T]))} for n in ("in", "out")}

    rot = [ps(f"maxima_scores{i}", [P, S]) for i in range(2)]
    work = ps("scores", [P, 4, S])
    cps = ps("contexts", [P, S])
    side = ps("side", [P, S])

    w_in = {n: sem(f"w{n}_in") for n in "qkvo"}
    b_in = sem("biases_in")
    w_split = sem("w_split")
    w_high = sem("w_high")
    b_scaled = sem("bias_q_scaled")
    q_scaled = sem("q_weight_scaled")
    const_a = sem("constants_made")
    const_v = sem("masks_made")
    x_in = sem("x_in")
    res_in = [sem(f"x_residual_in{i}") for i in range(2)]
    ln_stat = {n: sem(f"ln_{n}_stat") for n in ("in", "out")}
    ln_step = {n: sem(f"ln_{n}_step") for n in ("in", "out")}
    ln_rstd = {n: sem(f"ln_{n}_rstd") for n in ("in", "out")}
    xn_ready = sem("xn_ready")
    side_full = sem("side_full")
    side_free = sem("side_free")
    xTh = sem("xT_high_ready")
    v_half = sem("v_half_copied")
    rot_full = sem("rot_full")
    rot_free = sem("rot_free")
    qk_h = sem("qk_high_ready")
    qk_m = sem("qk_middle_ready")
    qk_l = sem("qk_low_ready")
    stack_in = [sem(f"stack_in{i}") for i in range(SETS)]
    max_step = sem("max_part_ready")
    max_ready = sem("max_parts_ready")
    m_in = [sem(f"max_rows_in{i}") for i in range(2)]
    st_full = sem("scores_full")
    p_full = sem("probs_ready")
    pv_done = sem("contexts_added")
    c0_out = sem("even_contexts_read")
    c1_out = sem("odd_contexts_read")
    den_sh = sem("denominators_shuffled")
    den_ln = sem("denominators_ln")
    den_rec = sem("denominators_inverted")
    den_one = sem("denominators_times_reciprocals")
    den_two = sem("reciprocal_factors_ready")
    den_fine = sem("reciprocals_refined")
    c_h = sem("ctx_high_ready")
    c_norm = sem("ctx_normalised")
    c_l = sem("ctx_low_ready")
    yn_ready = sem("y_normalised")
    r_ready = sem("row_sum_ready")
    rows_out = sem("rows_out")

    PROBS0, PV0, ODD0, SHUF0, LOW0, OUT0 = 2, 2, 1, 1, 1, 16

    def unit(h):
        return [("t", h // GH - 1)] * (h % GH == 0 and h > 0) + [("s", h // GH, h % GH, qc) for qc in range(T)] * (h < NH)

    rot_items = [item for h in range(NH + 1) for item in unit(h)]
    rot_at = {item: i for i, item in enumerate(rot_items)}
    ROT = len(rot_items)
    assert ROT % 2 == 0

    rot_count = [5 if n in (4, 5, 6, 7, 12, 19, 20, 28, 29, 30, 31) else 3 if n in (9, 24, 25) else 4 for n in range(STEPS)]
    assert sum(rot_count) == ROT

    def rot_step(n, last):
        lo = sum(len(unit(h)) for h in range(LEAD)) + sum(rot_count[:n])
        both = [(i, 0) for i in rot_items] + [(i, 1) for i in rot_items] * (not last)
        return both[lo:lo + rot_count[n]]

    ahead = [("x", t) for t in range(T)] + [("q", 0), ("k", 0), ("q", 1), ("k", 1), ("v", 0), ("v", 1), ("v", 2)]
    side_steps = {0: ("v", 3, 0, 2), 1: ("v", 3, 2, 4), 2: ("q", 2, 0, 2), 3: ("q", 2, 2, 4), 4: ("k", 2, 0, 4),
                  5: ("o", 0, 0, 4), 6: ("o", 1, 0, 4), 7: ("o", 2, 0, 4), 8: ("o", 3, 0, 4),
                  10: ("q", 3, 0, 2), 11: ("q", 3, 2, 4), 12: ("k", 3, 0, 4),
                  14: ("x", 0, 0, 4), 15: ("x", 1, 0, 4), 16: ("x", 2, 0, 4), 17: ("x", 3, 0, 4),
                  18: ("q", 0, 0, 2), 19: ("q", 0, 2, 4), 20: ("k", 0, 0, 4),
                  26: ("q", 1, 0, 2), 27: ("q", 1, 2, 4), 28: ("k", 1, 0, 4),
                  29: ("v", 0, 0, 4), 30: ("v", 1, 0, 4), 31: ("v", 2, 0, 4)}
    side_ends = {n: (what, i) for n, (what, i, _, last) in side_steps.items() if last == KC}
    side_items = ahead + [i for n, i in sorted(side_ends.items()) if i not in ahead]
    side_at = {item: i for i, item in enumerate(side_items)}
    SIDE = len(side_items)

    start = ([("w", "q")] + [("x", t) for t in range(T)] + [("w", "k"), ("q", 0), ("w", "v"), ("k", 0), ("w", "o")]
             + [("v", 0), ("v", 1), ("v", 2)]
             + [("r", h) for h in range(GH - 1)] + [("q", 1), ("k", 1)] + [("r", h) for h in range(GH - 1, LEAD)])
    start_at = {item: i for i, item in enumerate(item for item in start if item[0] not in "rw")}
    assert len(start_at) == len(ahead) and all(start_at[item] <= side_at[item] for item in ahead if item[0] == "v")

    def side_step(n, last):
        what, i, lo, hi = side_steps.get(n, (None, 0, 0, 0))
        return (None, 0, 0, 0) if last and of_next((what, i), n) else (what, i, lo, hi)

    def side_end(n, last):
        item = side_ends.get(n)
        return None if last and item and of_next(item, n) else item

    def of_next(item, n):
        return 1 if item in ahead and n >= 14 else 0

    fill_steps = {(4 * g - 11) % STEPS: g for g in range(G)}

    def filled(n, g):
        return (n * (G // SETS) + g // SETS + 1) * FILL

    def slots(g):
        s = g % SETS
        return slice(s * GH, s * GH + GH)

    turns.close()
    rounding = weight_rounding(nc, ctx, *ffn_weights)
    EARLY = 5
    BEFORE = EARLY + 4
    BESIDE = BEFORE + T
    shared = Shared()
    shared.rounding, shared.rounded, shared.minus_half = rounding, BESIDE, minus_half
    shared.side_free, shared.side_items = side_free, B * SIDE + T
    shared.rows_out, shared.rows_before_last = rows_out, OUT0 + B * T * 16

    @block.sync
    def _(sp):
        def load_weight(n, W, slot):
            dst = probs[:, slot]
            if n == "o":
                v = W.rearrange("(o e j d) n -> j e d o n", o=O, e=2, j=GH)
                for j in range(GH):
                    for e in range(2):
                        lo = 32 * j + D * e
                        sp.dma_start(dst[lo:lo + D, :, :], v[j, e]).then_inc(w_in[n], 16)
            else:
                sp.dma_start(dst, W.rearrange("(c p) n -> p c n", p=P)).then_inc(w_in[n], 16)

        def load_x(n):
            sp.dma_start(x_rows[:], x[n % B].rearrange("(t p) h -> p t h", p=P)).then_inc(x_in, 16)

        load_x(0)
        load_weight("q", Wq, 0)
        load_weight("k", Wk, 1)
        for i, bias in enumerate((bq, bk)):
            v = bias.rearrange("(o g h d) -> g h d o", o=O, g=2, h=GH)
            for g in range(2):
                for h in range(GH):
                    rows = slice(64 * g + h, 64 * g + 64, GH)
                    sp.dma_start(b_qk[rows, i, :], v[g, h], allow_slow_non_contiguous=True).then_inc(b_in, 16)
        sp.dma_start(bv_rows[:], bv.partition_broadcast(P)).then_inc(b_in, 16)
        sp.dma_start(bo_rows[:], bo.partition_broadcast(P)).then_inc(b_in, 16)
        sp.wait_ge(w_split, 1)
        load_weight("v", Wv, 0)
        sp.wait_ge(w_split, 2)
        load_weight("o", Wo, 1)

        def fill(n, g):
            half = slice(64 * (g % 2), 64 * (g % 2) + 64)
            sp.wait_ge(qk_l, (n * O + g // 2) * 2 + 2)
            sp.dma_start(q_st[96:99, slots(g), :], k_st[112:115, slots(g), :]).then_inc(stack_in[g % SETS], 16)
            for r, (qp, kp) in enumerate(PRODUCTS):
                rows = slice(D * r, D * r + D)
                sp.dma_start(q_st[rows, slots(g), :], qkT[half, qp, :]).then_inc(stack_in[g % SETS], 16)
                sp.dma_start(k_st[rows, slots(g), :], qkT[half, 3 + kp, :]).then_inc(stack_in[g % SETS], 16)

        def max_rows(n, g):
            sp.wait_ge(max_ready, n * G + g + 1)
            for r in range(3):
                sp.dma_start(q_st[96 + r:97 + r, slots(g), :], max_part[:, g % 2, r, :]).then_inc(m_in[g % 2], 16)

        def send_rows(n, t):
            sp.wait_ge(r_ready, n * T + t + 1)
            sp.dma_start(middle[n, t * P:t * P + P, :], y[:, t, :]).then_inc(rows_out, 16)

        def load_residual(n, t):
            if t >= 2:
                sp.wait_ge(r_ready, n * T + t - 1)
            sp.dma_start(x_res[:, t % 2, :], x[(n + B - 1) % B, t * P:t * P + P, :]).then_inc(res_in[t % 2], 16)

        sp.wait_ge(const_a, STACKS_CLEAR)
        fill(0, 0)
        fill(0, 1)
        sp.wait_ge(side_full, side_at[("x", T - 1)] + 1)
        load_x(1)
        max_rows(0, 0)
        fill(0, 2)

        def turn(b, last):
            for n in range(STEPS):
                if n % T == 1:
                    rows = ((n // T + 1) // G, (n // T + 1) % G)
                    g = fill_steps[n]
                    if g % 2 == 0 and not (last and rows[0]):
                        max_rows(b + rows[0], rows[1])
                    if not (last and n >= 21):
                        sp.wait_ge(st_full, (b * STEPS + max(n - 1, 1)) * 2)
                        fill(b + (1 if n >= 21 else 0), g)
                    if g % 2:
                        max_rows(b + rows[0], rows[1])
                if n == 6:
                    load_residual(b, 0)
                    load_residual(b, 1)
                if n == 15:
                    load_residual(b, 2)
                    load_residual(b, 3)
                    send_rows(b, 0)
                    send_rows(b, 1)
                if n == 19:
                    send_rows(b, 2)
                    send_rows(b, 3)
                if n == 22 and last:
                    sp.wait_ge(side_free, B * SIDE)
                    sp.wait_ge(qk_l, B * O * 2)
                    for g in range(G - 2, G):
                        sp.wait_ge(stack_in[g % SETS], filled(b, g))
                    sp.wait_ge(x_in, (B + 1) * 16)
                    for i in range(min(BESIDE, rounding.RAW)):
                        rounding.load(sp, i)
                if n == 19 and not last:
                    sp.wait_ge(side_full, (b + 1) * SIDE + side_at[("x", T - 1)] + 1)
                    load_x(b + 2)

        with sp.Fori(0, B - 1) as b:
            turn(b, False)
        turn(B - 1, True)
        load_residual(B, 0)
        load_residual(B, 1)
        sp.wait_ge(pv_done, PV0 + B * STEPS)
        sp.wait_ge(rot_free, B * ROT)
        for i in range(rounding.RAW, BESIDE):
            rounding.load(sp, i)

        def last_rows():
            for t in range(T):
                if t < T - 2:
                    load_residual(B, t + 2)
                send_rows(B, t)
            sp.wait_ge(rows_out, OUT0 + (B + 1) * T * 16)

        shared.last_rows = last_rows

    @block.gpsimd
    def _(pool):
        def inverse_std(name, n):
            a = norms[name]
            pool.wait_ge(ln_step[name], (n + 1) * AGGR)
            pool.tensor_tensor(a["rstd"][:], a["varpe"][:], minus_half[:], ALU.pow).then_inc(ln_rstd[name], 1)

        pool.memset(ident[:], 0.0).then_inc(const_a, 1)
        pool.wait_ge(const_a, 1)
        pool.affine_select(out=ident[:], in_=ident[:], compare_op=ALU.not_equal, fill=1.0, base=0,
                           pattern=[[-1, P]], channel_multiplier=1).then_inc(const_a, 1)
        pool.memset(minus_half[:], -0.5).then_inc(const_a, 1)
        pool.memset(two[:], 2.0).then_inc(const_a, 1)
        pool.wait_ge(const_a, 4)
        inverse_std("in", 0)
        pool.memset(q_st[:], 0.0).then_inc(const_a, 1)
        pool.memset(k_st[:], 0.0).then_inc(const_a, 1)
        pool.wait_ge(const_a, 6)
        pool.memset(k_st[96:99], -1.0).then_inc(const_a, 1)

        def project_low(n, what, o):
            i = (n * O + o) * 2 + "qk".index(what)
            part = 3 * "qk".index(what)
            pool.wait_ge(qk_m, i + 1)
            pool.tensor_tensor(qkT[:, part + 2, :], qk_rest[:], qkT[:, part + 1, :], ALU.subtract).then_inc(qk_l, 1)

        def times_reciprocal(k, o):
            pool.wait_ge(den_rec, k + 1)
            pool.tensor_tensor(den[:, o % 2, :], den[:, o % 2, :], rec[:], ALU.mult).then_inc(den_one, 1)

        def normalise(k, o, last_use):
            if last_use is not None:
                pool.wait_ge(side_full, last_use)
            pool.wait_ge(den_two, k + 1)
            pool.tensor_tensor(den[:, o % 2, :], den[:, o % 2, :], rec[:], ALU.mult).then_inc(den_fine, 1)
            pool.wait_ge(den_fine, k + 1)
            pool.tensor_tensor(cT_h[:, o, :], ctx_raw[:, o % 2, :], den[:, o % 2, :], ALU.mult).then_inc(c_h, 1)
            pool.wait_ge(c_h, k + 1)
            pool.tensor_tensor(ctx_raw[:, o % 2, :], ctx_raw[:, o % 2, :], den[:, o % 2, :], ALU.mult).then_inc(c_norm, 1)
            pool.wait_ge(c_norm, k + 1)
            pool.tensor_tensor(cT_l[:, o, :], ctx_raw[:, o % 2, :], cT_h[:, o, :].bitcast(F32), ALU.subtract).then_inc(c_l, 1)

        def add_residual(n, t):
            pool.wait_ge(yn_ready, n * T + t + 1)
            pool.wait_ge(res_in[t % 2], (n * 2 + t // 2 + 1) * 16)
            pool.tensor_tensor(y[:, t, :], y[:, t, :], x_res[:, t % 2, :], ALU.add).then_inc(r_ready, 1)

        pool.wait_ge(const_a, STACKS_CLEAR)
        pool.memset(v_one[:], 1.0).then_inc(const_a, 1)
        for item in start:
            if item[0] in "qk":
                project_low(0, *item)
            if item == ("k", 0):
                pool.memset(cT_h[:].bitcast(F32), 0.0).then_inc(const_a, 1)
                pool.memset(cT_l[:].bitcast(F32), 0.0).then_inc(const_a, 1)
                pool.memset(ctx_raw[:], 0.0).then_inc(const_a, 1)
                pool.memset(den[:], 1.0).then_inc(const_a, 1)
        pool.wait_ge(const_a, CONSTS)

        def turn(b, last):
            for n in range(STEPS):
                if n == 11:
                    inverse_std("out", b)
                if n == 1:
                    times_reciprocal(b * O, O - 1)
                if n == 2:
                    normalise(b * O, O - 1, None)
                if n % 8 == 2 and n > 2:
                    times_reciprocal(b * O + n // 8, n // 8 - 1)
                if n > 8 and n % 8 == (4 if last else 3):
                    o = n // 8 - 1
                    normalise(b * O + 1 + o, o, b * SIDE + side_at[("o", T - 1)] + 1 if o == 0 else None)
                before = side_end(n - 1, last)
                if before and before[0] in "qk":
                    project_low(b + of_next(before, n - 1), *before)
                if n == 5 and not last:
                    inverse_std("in", b + 1)
                if 13 <= n < 13 + T:
                    add_residual(b, n - 13)
                if last and n >= STEPS - EARLY:
                    rounding.take_magic(pool, n - (STEPS - EARLY))

        with pool.Fori(0, B - 1) as b:
            turn(b, False)
        turn(B - 1, True)
        times_reciprocal(B * O, O - 1)
        normalise(B * O, O - 1, None)
        for i in range(EARLY, BESIDE):
            rounding.take_magic(pool, i)

        def last_residual():
            for t in range(T):
                add_residual(B, t)

        shared.last_inverse_std = lambda: inverse_std("out", B)
        shared.last_residual = last_residual

    @block.scalar
    def _(act):
        act.sem_inc(p_full, PROBS0)
        act.preload_act_table_set("natural_log_exp_and_others")

        def weight_high(n):
            i = "qkvo".index(n)
            if n == "q":
                act.wait_ge(q_scaled, 1)
            else:
                act.wait_ge(w_in[n], 128 if n == "o" else 16)
            for c in range(KC):
                src, dst = probs[:, i % 2, c, :], w_h[n][:, c, :]
                if n in "qk":
                    src = src.rearrange("p (a h d) -> p a d h", h=GH, d=D)
                    dst = dst.rearrange("p (a d h) -> p a d h", h=GH, d=D)
                act.copy(dst, src).then_inc(w_high, 1)

        def side_high(n, item, at):
            what, i = item
            if what not in "xqk":
                return
            act.wait_ge(side_full, at + 1)
            if what == "x":
                act.copy(xT_h[:, :, i * P:i * P + P], side[:].rearrange("p (c t) -> p c t", c=KC)).then_inc(xTh, 1)
                return
            for g in (2 * i - 2, 2 * i - 1):
                if g >= 0:
                    act.wait_ge(stack_in[g % SETS], filled(n, g))
                elif not (isinstance(n, int) and n == 0):
                    act.wait_ge(stack_in[g % SETS], filled(n - 1, g + G))
            part = 3 * "qk".index(what)
            act.activation(qkT[:, part, :], side[:], ACT.Identity, bias=b_qk[:, part // 3, i:i + 1]).then_inc(qk_h, 1)

        def side_middle(item, at):
            what, i = item
            if what in "qk":
                part = 3 * "qk".index(what)
                act.wait_ge(side_free, at + 1)
                act.copy(qkT[:, part + 1, :], qk_rest[:]).then_inc(qk_m, 1)

        def contexts_even(b, o):
            act.wait_ge(pv_done, PV0 + b * STEPS + (2 * o + 1) * T)
            act.wait_ge(c_l, LOW0 + b * O + o)
            act.mul(ctx_raw[:, o % 2, :], cps[:], half_mask[:, 0:1]).then_inc(c0_out, 1)
            act.mul(den[:, o % 2, :], cps[:], half_mask[:, 1:2]).then_inc(c0_out, 1)

        def invert(k, o):
            act.wait_ge(den_sh, SHUF0 + k)
            act.wait_ge(c_l, LOW0 + k)
            act.activation(rec[:], den[:, o % 2, :], ACT.Ln).then_inc(den_ln, 1)
            act.wait_ge(den_ln, k + 1)
            act.activation(rec[:], rec[:], ACT.Exp, scale=-1.0).then_inc(den_rec, 1)

        def refine(k, o):
            act.wait_ge(den_one, k + 1)
            act.activation(den[:, o % 2, :], den[:, o % 2, :], ACT.Identity, bias=two[:], scale=-1.0).then_inc(den_two, 1)

        for item in start:
            if item[0] == "w":
                weight_high(item[1])
                if item[1] == "k":
                    act.wait_ge(b_in, 16 * (4 * GH + 2))
                    act.mul(b_qk[:, 0, :], b_qk[:, 0, :], float(D) ** -0.5).then_inc(b_scaled, 1)
                    act.wait_ge(b_scaled, 1)
            elif item in start_at:
                side_high(0, item, start_at[item])
                side_middle(item, start_at[item])
        act.wait_ge(const_v, 1)
        act.wait_ge(const_a, CONSTS)

        def turn(b, last):
            for n in range(STEPS):
                g, c = divmod(n, T)
                before = side_end(n - 1, last)
                if before:
                    k = b + of_next(before, n - 1)
                    side_high(k, before, k * SIDE + side_at[before])
                if n == 1:
                    invert(b * O, O - 1)
                if n == 2:
                    refine(b * O, O - 1)
                if n % 8 == 2 and n > 2:
                    invert(b * O + n // 8, n // 8 - 1)
                if n > 8 and n % 8 == (4 if last else 3):
                    refine(b * O + n // 8, n // 8 - 1)
                for u in range(2):
                    act.wait_ge(st_full, (b * STEPS + n) * 2 + u + 1)
                    act.wait_ge(pv_done, PV0 + b * STEPS + n - 1)
                    act.activation(probs[:, n % 2, 2 * u:2 * u + 2, :], work[:, 2 * u:2 * u + 2, :], ACT.Exp).then_inc(p_full, 1)
                if before:
                    side_middle(before, k * SIDE + side_at[before])
                if n % 8 == 4:
                    contexts_even(b, n // 8)
                if last and n > STEPS - EARLY:
                    rounding.overflow(act, n - (STEPS - EARLY) - 1)

        with act.Fori(0, B - 1) as b:
            turn(b, False)
        turn(B - 1, True)
        invert(B * O, O - 1)
        refine(B * O, O - 1)
        for i in range(EARLY - 1, BESIDE):
            rounding.overflow(act, i)

    @block.vector
    def _(dve):
        dve.wait_ge(const_a, 2)
        dve.tensor_reduce(half_mask[:], ident[:].rearrange("p (j e d) -> p e j d", j=GH, e=2), AX.XY, ALU.add).then_inc(const_v, 1)
        dve.sem_inc(c1_out, ODD0)
        dve.sem_inc(den_sh, SHUF0)

        def weight_low(n):
            i = "qkvo".index(n)
            for c in range(KC):
                dve.wait_ge(w_high, i * KC + c + 1)
                src, high, dst = probs[:, i % 2, c, :], w_h[n][:, c, :].bitcast(F32), w_l[n][:, c, :]
                if n in "qk":
                    src = src.rearrange("p (a h d) -> p a d h", h=GH, d=D)
                    high, dst = (a.rearrange("p (a d h) -> p a d h", h=GH, d=D) for a in (high, dst))
                last = dve.tensor_tensor(dst, src, high, ALU.subtract)
            last.then_inc(w_split, 1)

        def stats(name, rows, t):
            dve.bn_stats(norms[name]["stats"][:, t, :], rows[:, t, :]).then_inc(ln_stat[name], 1)

        def moments(name, n):
            a = norms[name]
            aggregate(dve, n, T, H, a["stats"], a["mean"], a["spread"], a["varpe"], ln_stat[name], ln_step[name])

        def normalise(name, rows, done, n, t):
            if t == 0:
                dve.wait_ge(ln_rstd[name], n + 1)
            dve.tensor_scalar(rows[:, t, :], rows[:, t, :], norms[name]["mean"][:, t:t + 1],
                              norms[name]["rstd"][:, t:t + 1], ALU.subtract, ALU.mult).then_inc(done, 1)

        def take(n, item, b=None):
            what, i = item
            at = start_at[item] if b is None else n * SIDE + side_at[item]
            if what == "x":
                dve.wait_ge(xTh, n * T + i + 1)
                toks = slice(i * P, i * P + P)
                dve.tensor_tensor(xT_l[:, :, toks], side[:].rearrange("p (c t) -> p c t", c=KC),
                                  xT_h[:, :, toks].bitcast(F32), ALU.subtract).then_inc(side_free, 1)
            elif what == "v":
                dve.wait_ge(side_full, at + 1)
                if b is not None:
                    dve.wait_ge(pv_done, PV0 + n * STEPS + i - T + 1)
                for e in range(2):
                    dst = v_one[:, i].rearrange("p (a e j) w -> p e a j w", e=2, j=GH)[:, e, :, :, e * D:e * D + D]
                    src, bias = (a.rearrange("p (a e j d) -> p e a j d", e=2, j=GH, d=D)[:, e] for a in (side[:], bv_rows[:]))
                    dve.tensor_tensor(dst, src, bias, ALU.add).then_inc((v_half, side_free)[e], 1)
            elif what == "o":
                take_out(at, n, i)
            else:
                k = (n * O + i) * 2 + "qk".index(what)
                part = 3 * "qk".index(what)
                dve.wait_ge(qk_h, k + 1)
                if not (isinstance(k, int) and k == 0):
                    dve.wait_ge(qk_l, k)
                dve.scalar_tensor_tensor(qk_rest[:], side[:], b_qk[:, part // 3, i:i + 1], qkT[:, part, :],
                                         ALU.add, ALU.subtract).then_inc(side_free, 1)

        def take_out(at, n, t):
            dve.wait_ge(side_full, at + 1)
            dve.wait_ge(rows_out, OUT0 + n * T * 16)
            dve.tensor_tensor(y[:, t, :], side[:], bo_rows[:], ALU.add).then_inc(side_free, 1)

        def reduce_maxima(n, item):
            at = n * ROT + rot_at[item]
            bank = rot[rot_at[item] % 2]
            dve.wait_ge(rot_full, at + 1)
            if item[0] == "s":
                _, g, j, qc = item
                dve.tensor_reduce(maxima[:, g % 2, j * T + qc:j * T + qc + 1], bank[:], AX.X, ALU.max).then_inc(rot_free, 1)
                return
            g = item[1]
            k = n * G + g
            rows = bank[0:GH * T, 0:P]
            if g >= 2:
                dve.wait_ge(m_in[g % 2], (n * (G // 2) + g // 2) * 48)
            elif not (isinstance(n, int) and n == 0):
                dve.wait_ge(m_in[g % 2], (n * (G // 2)) * 48) if g == 0 else dve.wait_ge(m_in[0], (n * (G // 2) + 1) * 48)
            dve.tensor_copy(max_part[:, g % 2, 0, :], rows).then_inc(max_step, 1)
            dve.wait_ge(max_step, k * 2 + 1)
            dve.tensor_tensor(max_rest[:], rows, max_part[:, g % 2, 0, :], ALU.subtract).then_inc(rot_free, 1)
            dve.wait_ge(rot_free, at + 1)
            dve.tensor_copy(max_part[:, g % 2, 1, :], max_rest[:]).then_inc(max_step, 1)
            dve.wait_ge(max_step, k * 2 + 2)
            dve.tensor_tensor(max_part[:, g % 2, 2, :], max_rest[:], max_part[:, g % 2, 1, :], ALU.subtract).then_inc(max_ready, 1)

        def denominators_odd(b, o):
            k = b * O + o
            dve.wait_ge(pv_done, PV0 + b * STEPS + (2 * o + 2) * T)
            dve.wait_ge(c0_out, (k + 1) * 2)
            dve.scalar_tensor_tensor(den[:, o % 2, :], cps[:], half_mask[:, 0:1], den[:, o % 2, :], ALU.mult, ALU.add).then_inc(c1_out, 1)

        def contexts_odd(b, o):
            k = b * O + o
            dve.wait_ge(c1_out, ODD0 + k * 2 + 1)
            dve.scalar_tensor_tensor(ctx_raw[:, o % 2, :], cps[:], half_mask[:, 1:2], ctx_raw[:, o % 2, :], ALU.mult, ALU.add).then_inc(c1_out, 1)

        def shuffle(o):
            dve.stream_shuffle(den[:, o % 2, :], den[:, o % 2, :], [(i + D) % 32 for i in range(32)]).then_inc(den_sh, 1)

        dve.wait_ge(x_in, 16)
        for t in range(T):
            stats("in", x_rows, t)
        moments("in", 0)
        dve.wait_ge(w_in["q"], 16)
        dve.tensor_scalar(probs[:, 0], probs[:, 0], float(D) ** -0.5, None, ALU.mult).then_inc(q_scaled, 1)
        for t in range(T):
            normalise("in", x_rows, xn_ready, 0, t)
        dve.wait_ge(q_scaled, 1)
        for item in start:
            if item[0] == "r":
                for i in unit(item[1]):
                    reduce_maxima(0, i)
            elif item[0] == "w":
                weight_low(item[1])
            else:
                if item == ("q", 0):
                    dve.wait_ge(b_scaled, 1)
                if item == ("v", 0):
                    dve.wait_ge(const_a, ONES)
                take(0, item)
        dve.wait_ge(const_a, CONSTS)

        def turn(b, last):
            for n in range(STEPS):
                items = rot_step(n, last)
                for k, (item, later) in enumerate(items):
                    reduce_maxima(b + later, item)
                    before = side_end(n - 1, last)
                    if k == 0 and before:
                        take(b + of_next(before, n - 1), before, b)
                    if k == 1 and before and before[0] == "o":
                        dve.wait_ge(side_free, b * SIDE + side_at[before] + 1)
                        stats("out", y, before[1])
                    if n in (1, 2) and k in (1, 2) and not last:
                        t = 2 * (n - 1) + k - 1
                        if t == 0:
                            dve.wait_ge(x_in, (b + 2) * 16)
                        stats("in", x_rows, t)
                    if n == 3 and k == 1 and not last:
                        moments("in", b + 1)
                    if n in (6, 7) and k in (2, 3) and not last:
                        normalise("in", x_rows, xn_ready, b + 1, 2 * (n - 6) + k - 2)
                    if n == 10 and k == 1:
                        moments("out", b)
                    if n in (11, 12) and k in (1, 2):
                        normalise("out", y, yn_ready, b, 2 * (n - 11) + k - 1)
                    if n % 8 == 0 and n and k == 1:
                        denominators_odd(b, n // 8 - 1)
                    if n % 8 == 0 and n and k == len(items) - 1:
                        contexts_odd(b, n // 8 - 1)
                    if n % 8 == 1 and n > 1 and k == 0:
                        shuffle(n // 8 - 1)
                if last and n >= STEPS - EARLY:
                    rounding.quantise(dve, n - (STEPS - EARLY))
            if not last:
                take(b + 1, ("v", 2), b)
            denominators_odd(b, O - 1)
            contexts_odd(b, O - 1)
            shuffle(O - 1)

        with dve.Fori(0, B - 1) as b:
            turn(b, False)
        turn(B - 1, True)
        for i in range(EARLY, BEFORE):
            rounding.quantise(dve, i)
        for t in range(T):
            take_out(B * SIDE + t, B, t)
            dve.wait_ge(side_free, B * SIDE + t + 1)
            stats("out", y, t)
            rounding.quantise(dve, BEFORE + t)

        def last_normalise():
            for t in range(T):
                normalise("out", y, yn_ready, B, t)

        shared.last_moments = lambda: moments("out", B)
        shared.last_normalise = last_normalise

    @block.tensor
    def _(pe):
        pe.sem_inc(pv_done, PV0)
        pe.sem_inc(c_l, LOW0)
        pe.sem_inc(rows_out, OUT0)
        pe.wait_ge(const_a, IDENT)

        def product(out, left, right, first, last):
            for i, (a, c) in enumerate(((0, 0), (1, 0), (0, 1))):
                mm = pe.matmul(out, left[a], right[c], start=first and i == 0, stop=last and i == 2)
            return mm

        def side_piece(at, n, item, c):
            what, i = item
            if c == 0 and not (isinstance(at, int) and at == 0):
                pe.wait_ge(side_free, at)
            toks = slice(i * P, i * P + P)
            if what == "x":
                if c == 0:
                    pe.wait_ge(xn_ready, n * T + i + 1)
                mm = pe.transpose(side[:, c * P:c * P + P], x_rows[:, i, c * P:c * P + P], ident[:])
            elif what in "qk":
                mm = product(side[:], (w_h[what][:, c, toks], w_l[what][:, c, toks]),
                             (xT_h[:, c, :], xT_l[:, c, :]), c == 0, c == KC - 1)
            elif what == "v":
                mm = product(side[:], (xT_h[:, c, toks], xT_l[:, c, toks]),
                             (w_h["v"][:, c, :], w_l["v"][:, c, :]), c == 0, c == KC - 1)
            else:
                if c == 0:
                    pe.wait_ge(c_l, LOW0 + n * O + 1)
                mm = product(side[:], (cT_h[:, c, toks], cT_l[:, c, toks]),
                             (w_h["o"][:, c, :], w_l["o"][:, c, :]), c == 0, c == KC - 1)
            if c == KC - 1:
                mm.then_inc(side_full, 1)

        def rot_item(n, item):
            at = n * ROT + rot_at[item]
            bank = rot[rot_at[item] % 2]
            if not (isinstance(at, int) and at < 2):
                pe.wait_ge(rot_free, at - 1)
            if item[0] == "s":
                _, g, j, qc = item
                if j == 0 and qc == 0:
                    pe.wait_ge(stack_in[g % SETS], filled(n, g))
                s = (g % SETS) * GH + j
                mm = pe.matmul(bank[:], q_st[:, s, qc * P:qc * P + P], k_st[:, s, :], start=True, stop=True)
            else:
                pe.wait_ge(rot_free, at)
                mm = pe.transpose(bank[0:GH * T, 0:P], maxima[:, item[1] % 2, :], ident[:])
            mm.then_inc(rot_full, 1)

        def scores(b, n, u):
            g, c = divmod(n, T)
            pe.wait_ge(p_full, PROBS0 + (b * STEPS + n) * 2 + u - 1)
            if c == 0 and u == 0:
                pe.wait_ge(m_in[g % 2], (b * (G // 2) + g // 2 + 1) * 48)
            for j in range(2 * u, 2 * u + 2):
                s = (g % SETS) * GH + j
                mm = pe.matmul(work[:, j, :], k_st[:, s, c * P:c * P + P], q_st[:, s, :], start=True, stop=True)
            mm.then_inc(st_full, 1)

        def contexts(b, n):
            g, c = divmod(n, T)
            pe.wait_ge(p_full, PROBS0 + (b * STEPS + n + 1) * 2)
            if g == 0:
                pe.wait_ge(side_free, b * SIDE + side_at[("v", c)] + 1)
            if c == 0:
                pe.wait_ge(*((c0_out, (b * O + g // 2 + 1) * 2) if g % 2 else (c1_out, ODD0 + (b * O + g // 2) * 2)))
            for j in range(GH):
                mm = pe.matmul(cps[32 * j:32 * j + 32, :], v_one[:, c, GH * g + j, :],
                               probs[:, n % 2, j, :], start=(c == 0), stop=(c == T - 1))
            mm.then_inc(pv_done, 1)

        for item in start:
            if item[0] == "r":
                for i in unit(item[1]):
                    rot_item(0, i)
            elif item in start_at:
                if item[0] in "qkv":
                    pe.wait_ge(w_split, "qkv".index(item[0]) + 1)
                for c in range(KC):
                    side_piece(start_at[item], 0, item, c)
        pe.wait_ge(w_split, 4)
        pe.wait_ge(const_a, CONSTS)

        def turn(b, last):
            for n in range(STEPS):
                items = rot_step(n, last)
                cut = [len(items) * k // 5 for k in range(5 + 1)]
                what, i, lo, hi = side_step(n, last)
                pieces = range(lo, hi)
                later = b + of_next((what, i), n)

                def share(k):
                    for item, nxt in items[cut[k]:cut[k + 1]]:
                        rot_item(b + nxt, item)

                def piece(k):
                    if k < len(pieces):
                        side_piece(later * SIDE + side_at[what, i], later, (what, i), pieces[k])

                share(0)
                scores(b, n, 0)
                share(1)
                scores(b, n, 1)
                share(2)
                if n:
                    contexts(b, n - 1)
                piece(0)
                share(3)
                piece(1)
                share(4)
                piece(2)
                piece(3)
            contexts(b, STEPS - 1)

        with pe.Fori(0, B - 1) as b:
            turn(b, False)
        turn(B - 1, True)
        for t in range(T):
            for c in range(KC):
                side_piece(B * SIDE + t, B, ("o", t), c)

    return shared


def ffn_pass(nc, ctx, block, shared, ident, middle, gate_s, up_s, down_s, out):
    B, S, H = out.shape
    T = S // P
    KC = H // P
    rounding = shared.rounding
    gate_q, up_q, down_q = rounding.gate_q, rounding.up_q, rounding.down_q
    F = rounding.F
    XS = 1024.0
    QF = rounding.QF

    sb = lambda name, shape, dt=F32: ctx.enter_context(nc.sbuf_tensor(name, shape, dt))
    ps = lambda name, shape: ctx.enter_context(nc.psum_tensor(name, shape, F32))
    sem = lambda name: ctx.enter_context(nc.semaphore(name))

    gs_in = sb("gate_scale_in", [P, F])
    us_in = sb("up_scale_in", [P, F])
    gs = sb("gate_scale", [P, F])
    us = sb("up_scale", [P, F])
    ds_rows = sb("down_scale_rows", [P, H])

    x_rows = sb("x_rows_ffn", [P, T, H])
    x_res = sb("x_residual_ffn", [P, T, H])
    y = sb("y_ffn", [P, T, H])
    xT_h = sb("xT_high_ffn", [P, KC, S], F16)
    xT_l = sb("xT_low_ffn", [P, KC, S], F16)
    gate = sb("gate", [P, 2, S])
    fuse = sb("fuse", [P, 2, S])
    fuse_h = sb("fuse_high", [P, 2, S], F32R)
    fuse_l = sb("fuse_low", [P, 2, S], F32R)
    norms = {n: {k: sb(f"{k}_{n}_ffn", s) for k, s in (("stats", [P, T, 6]), ("mean", [P, T]), ("spread", [P, 3, T]),
                                                       ("varpe", [P, T]), ("rstd", [P, T]))} for n in ("in", "out")}

    ring = ps("ring", [P, 2, 2, S])
    acc = ps("down_sums", [P, T, H])

    s_in = sem("scales_in")
    s_ready = sem("scales_ready")
    x_in = sem("x_in_ffn")
    res_in = sem("x_residual_in_ffn")
    ln_stat = {n: sem(f"ln_{n}_stat_ffn") for n in ("in", "out")}
    ln_step = {n: sem(f"ln_{n}_step_ffn") for n in ("in", "out")}
    ln_rstd = {n: sem(f"ln_{n}_rstd_ffn") for n in ("in", "out")}
    xn_ready = sem("xn_ready_ffn")
    xT_full = sem("xT_in_ring")
    xTh = sem("xT_high_ready_ffn")
    xTl = sem("xT_low_ready_ffn")
    gu_full = sem("gate_up_in_ring")
    silu = sem("gate_ready")
    fused = sem("fuse_ready")
    fh = sem("fuse_high_ready")
    fl = sem("fuse_low_ready")
    down_done = sem("down_added")
    y_ready = sem("y_ready_ffn")
    yn_ready = sem("y_normalised_ffn")
    r_ready = sem("row_sum_ready_ffn")
    rows_out = sem("rows_out_ffn")

    START = shared.rounded + 2
    assert START >= rounding.gate_up_jobs[0] + 2

    def jobs_at(f):
        lo = START + f * 3
        return range(min(lo, rounding.count), min(lo + 3, rounding.count))

    assert jobs_at(F - 1).stop == rounding.count and jobs_at(QF - 1).stop >= rounding.gate_up_jobs[1] + 2

    @block.sync
    def _(sp):
        sp.wait_ge(shared.rows_out, shared.rows_before_last)
        sp.dma_start(x_rows[:], middle[1].rearrange("(t p) h -> p t h", p=P)).then_inc(x_in, 16)
        sp.dma_start(gs_in[:], gate_s.rearrange("(f p) -> p f", p=P), allow_slow_non_contiguous=True).then_inc(s_in, 16)
        sp.dma_start(us_in[:], up_s.rearrange("(f p) -> p f", p=P), allow_slow_non_contiguous=True).then_inc(s_in, 16)
        sp.dma_start(ds_rows[:], down_s.partition_broadcast(P)).then_inc(s_in, 16)

        def load_x(n):
            sp.wait_ge(xT_full, (n + 1) * KC)
            sp.dma_start(x_rows[:], middle[(n + 1) % B + 1].rearrange("(t p) h -> p t h", p=P)).then_inc(x_in, 16)

        def end_rows(n):
            sp.dma_start(x_res[:], middle[n + 1].rearrange("(t p) h -> p t h", p=P)).then_inc(res_in, 16)
            for t in range(T):
                sp.wait_ge(r_ready, n * T + t + 1)
                sp.dma_start(out[n, t * P:t * P + P, :], y[:, t, :]).then_inc(rows_out, 16)

        room = shared.rounded + rounding.RAW
        for i in range(shared.rounded, room):
            rounding.load(sp, i)
        shared.last_rows()
        load_x(0)
        for i in range(room, rounding.count):
            rounding.load(sp, i)
        with sp.Fori(1, B) as b:
            load_x(b)
            end_rows(b - 1)
        end_rows(B - 1)
        sp.wait_ge(rows_out, B * T * 16)
        sp.wait_ge(x_in, (B + 1) * 16)

    @block.gpsimd
    def _(pool):
        def inverse_std(name, n):
            pool.wait_ge(ln_step[name], (n + 1) * AGGR)
            pool.tensor_tensor(norms[name]["rstd"][:], norms[name]["varpe"][:], shared.minus_half[:], ALU.pow).then_inc(ln_rstd[name], 1)

        def batch(b, first):
            for f in range(F):
                if first:
                    for i in jobs_at(f):
                        rounding.take_magic(pool, i)
                elif f == 2:
                    inverse_std("out", b - 1)
                if f == 7:
                    inverse_std("in", b + 1)
                pool.wait_ge(fh, b * F + f + 1)
                pool.tensor_tensor(fuse_l[:, f % 2, :], fuse[:, f % 2, :], fuse_h[:, f % 2, :].bitcast(F32), ALU.subtract).then_inc(fl, 1)

        inverse_std("in", 0)
        rounding.take_magic(pool, shared.rounded)
        shared.last_inverse_std()
        for i in range(shared.rounded + 1, START):
            rounding.take_magic(pool, i)
        shared.last_residual()
        batch(0, True)
        with pool.Fori(1, B) as b:
            batch(b, False)
        inverse_std("out", B - 1)

    @block.scalar
    def _(act):
        def x_high(n):
            for c in range(KC):
                act.wait_ge(xT_full, n * KC + c + 1)
                act.mul(xT_h[:, c, :], ring[:, c // 2, c % 2, :], XS).then_inc(xTh, 1)

        def batch(b, first):
            for f in range(F):
                k = b * F + f
                chunks = jobs_at(f) if first else ()
                for i in chunks[:-1]:
                    rounding.overflow(act, i)
                act.wait_ge(gu_full, k * 2 + 1)
                act.activation(gate[:, f % 2, :], ring[:, f % 2, 0, :], ACT.Silu, scale=gs[:, f:f + 1]).then_inc(silu, 1)
                for i in chunks[-1:]:
                    rounding.overflow(act, i)
                act.wait_ge(fused, k + 1)
                if not first or f >= 2:
                    act.wait_ge(down_done, k - 1)
                act.copy(fuse_h[:, f % 2, :], fuse[:, f % 2, :]).then_inc(fh, 1)
            x_high(b + 1)

        act.preload_act_table(ACT.Silu)
        for i in range(shared.rounded, START):
            rounding.overflow(act, i)
        x_high(0)
        act.wait_ge(s_ready, 2)
        batch(0, True)
        with act.Fori(1, B) as b:
            batch(b, False)

    @block.vector
    def _(dve):
        def stats(name, rows, n):
            for t in range(T):
                if name == "out":
                    dve.wait_ge(y_ready, n * T + t + 1)
                dve.bn_stats(norms[name]["stats"][:, t, :], rows[:, t, :]).then_inc(ln_stat[name], 1)

        def moments(name, n):
            a = norms[name]
            aggregate(dve, n, T, H, a["stats"], a["mean"], a["spread"], a["varpe"], ln_stat[name], ln_step[name])

        def normalise(name, rows, done, n):
            dve.wait_ge(ln_rstd[name], n + 1)
            for t in range(T):
                dve.tensor_scalar(rows[:, t, :], rows[:, t, :], norms[name]["mean"][:, t:t + 1],
                                  norms[name]["rstd"][:, t:t + 1], ALU.subtract, ALU.mult).then_inc(done, 1)

        def add_residual(n):
            dve.wait_ge(res_in, (n + 1) * 16)
            for t in range(T):
                dve.wait_ge(yn_ready, n * T + t + 1)
                dve.tensor_tensor(y[:, t, :], y[:, t, :], x_res[:, t, :], ALU.add).then_inc(r_ready, 1)

        def x_low(n):
            for c in range(KC):
                dve.wait_ge(xTh, n * KC + c + 1)
                dve.scalar_tensor_tensor(xT_l[:, c, :], ring[:, c // 2, c % 2, :], XS, xT_h[:, c, :],
                                         ALU.mult, ALU.subtract).then_inc(xTl, 1)

        def batch(b, first):
            for f in range(F):
                k = b * F + f
                if first:
                    for i in jobs_at(f):
                        rounding.quantise(dve, i)
                elif f == 1:
                    stats("out", y, b - 1)
                    moments("out", b - 1)
                elif f == 3:
                    normalise("out", y, yn_ready, b - 1)
                    add_residual(b - 1)
                if f == 5:
                    dve.wait_ge(x_in, (b + 2) * 16)
                    stats("in", x_rows, b + 1)
                if f == 6:
                    moments("in", b + 1)
                if f == 8:
                    normalise("in", x_rows, xn_ready, b + 1)
                dve.wait_ge(gu_full, k * 2 + 2)
                dve.wait_ge(silu, k + 1)
                if not first or f >= 2:
                    dve.wait_ge(fl, k - 1)
                dve.scalar_tensor_tensor(fuse[:, f % 2, :], ring[:, f % 2, 1, :], us[:, f:f + 1], gate[:, f % 2, :],
                                         ALU.mult, ALU.mult).then_inc(fused, 1)
            x_low(b + 1)
            dve.wait_ge(down_done, (b + 1) * F)
            if not first:
                dve.wait_ge(rows_out, b * T * 16)
            for t in range(T):
                dve.tensor_tensor(y[:, t, :], acc[:, t, :], ds_rows[:], ALU.mult).then_inc(y_ready, 1)

        dve.wait_ge(x_in, 16)
        stats("in", x_rows, 0)
        moments("in", 0)
        rounding.quantise(dve, shared.rounded)
        normalise("in", x_rows, xn_ready, 0)
        shared.last_moments()
        for i in range(shared.rounded + 1, START):
            rounding.quantise(dve, i)
        dve.wait_ge(s_in, 48)
        dve.tensor_scalar(gs[:], gs_in[:], 1.0 / XS, None, ALU.mult).then_inc(s_ready, 1)
        dve.tensor_scalar(us[:], us_in[:], 1.0 / XS, None, ALU.mult).then_inc(s_ready, 1)
        shared.last_normalise()
        x_low(0)
        batch(0, True)
        with dve.Fori(1, B) as b:
            batch(b, False)
        stats("out", y, B - 1)
        moments("out", B - 1)
        normalise("out", y, yn_ready, B - 1)
        add_residual(B - 1)

    @block.tensor
    def _(pe):
        def transposes(n, half, first):
            if half == 0:
                pe.wait_ge(xn_ready, (n + 1) * T)
            if not first:
                pe.wait_ge(fused, n * F - 1 + half)
            for c in (2 * half, 2 * half + 1):
                for t in range(T):
                    mm = pe.transpose(ring[:, half, c % 2, t * P:t * P + P], x_rows[:, t, c * P:c * P + P], ident[:])
                mm.then_inc(xT_full, 1)

        def gate_up(b, f, first):
            k = b * F + f
            if first and f % QF == 0:
                pe.wait_ge(rounding.quant, rounding.gate_up_jobs[f // QF])
            if f == 0:
                pe.wait_ge(xTl, (b + 1) * KC)
            elif f >= 2:
                pe.wait_ge(fused, k - 1)
            for w, weight in enumerate((gate_q, up_q)):
                for c in range(KC):
                    for i, part in enumerate((xT_h, xT_l)):
                        mm = pe.matmul(ring[:, f % 2, w, :], weight[:, c, f * P:f * P + P], part[:, c, :],
                                       start=(c == 0 and i == 0), stop=(c == KC - 1 and i == 1))
                mm.then_inc(gu_full, 1)

        def down(b, f, first):
            if first:
                pe.wait_ge(rounding.quant, rounding.down_job[f])
                if f == 0:
                    pe.wait_ge(shared.side_free, shared.side_items)
            elif f == 0:
                pe.wait_ge(y_ready, b * T)
            pe.wait_ge(fl, b * F + f + 1)
            for t in range(T):
                toks = slice(t * P, t * P + P)
                for i, part in enumerate((fuse_h, fuse_l)):
                    mm = pe.matmul(acc[:, t, :], part[:, f % 2, toks], down_q[:, f, :],
                                   start=(f == 0 and i == 0), stop=(f == F - 1 and i == 1))
            mm.then_inc(down_done, 1)

        def batch(b, first):
            for f in range(F):
                gate_up(b, f, first)
                if 0 < f < F - 1:
                    down(b, f - 1, first)
            transposes(b + 1, 0, False)
            down(b, F - 2, first)
            transposes(b + 1, 1, False)
            down(b, F - 1, first)

        transposes(0, 0, True)
        transposes(0, 1, True)
        batch(0, True)
        with pe.Fori(1, B) as b:
            batch(b, False)


_INS = ['L0_attn_hidden_states', 'L0_attn_Wq', 'L0_attn_bq', 'L0_attn_Wk', 'L0_attn_bk', 'L0_attn_Wv', 'L0_attn_bv',
        'L0_attn_Wo', 'L0_attn_bo', 'L0_ffn_gate_w', 'L0_ffn_up_w', 'L0_ffn_down_w', 'L0_ffn_gate_scale',
        'L0_ffn_up_scale', 'L0_ffn_down_scale']


def kernel(**inputs):
    import numpy as np
    import concourse.bacc as bacc
    from concourse.bass_utils import run_bass_kernel_spmd

    nc = bacc.Bacc("TRN2", target_bir_lowering=False, num_devices=1)
    arrays, args = {}, []
    for name in _INS:
        a = np.ascontiguousarray(inputs[name])
        arrays[f"in_{name}"] = a
        args.append(nc.dram_tensor(f"in_{name}", a.shape, mybir.dt.from_np(a.dtype), kind="ExternalInput").ap())
    shape = inputs[_INS[0]].shape
    out = nc.dram_tensor("out_rows", shape, F32, kind="ExternalOutput").ap()
    layer(nc, *args, out)
    r = run_bass_kernel_spmd(nc, [arrays], core_ids=[0])
    return r.results[0]["out_rows"]
```
